# Optimizing a Trainium2 kernel written in Bass

```python
import numpy as np
import jax
import jax.numpy as jnp

def _softmax(x, axis=-1):
    return jax.nn.softmax(x, axis=axis)

def _gelu(x):
    return jax.nn.gelu(x, approximate=True)

def _silu(x):
    return jax.nn.silu(x)

def _sigmoid(x):
    return jax.nn.sigmoid(x)

def _layernorm(x, axis=-1, eps=1e-05):
    m = jnp.mean(x, axis=axis, keepdims=True)
    v = jnp.var(x, axis=axis, keepdims=True)
    return (x - m) / jnp.sqrt(v + eps)

def _scatter_add(tgt, idx, src, axis=0):
    return tgt.at[idx].add(src)

def _segment_sum(src, seg, n):
    return jax.ops.segment_sum(src, seg, n)
kernel_name = 'mk_adj_preln_d4_adj_r2_18eaa3'

def setup_inputs(seed: int=0):
    np.random.seed(seed)
    _w = jnp.asarray

    def _rec_inputs():
        import jax
        import jax.numpy as jnp
        _gk = jax.random.key(seed)
        x = -0.0005207 + 1.001 * jax.random.normal(jax.random.fold_in(_gk, 1), (64, 128, 128), jnp.float32)
        _a = jax.random.bernoulli(jax.random.fold_in(_gk, 2), 0.0625, (64, 128, 128))
        _a = jnp.logical_or(_a, jnp.eye(128, dtype=bool))
        _af = _a.astype(jnp.float32)
        _af = _af * jax.random.uniform(jax.random.fold_in(_gk, 3), (64, 128, 128), jnp.float32, 0.05, 1)
        adj = _af
        _nm = jnp.ones((64, 128), dtype=bool)
        nodemask = jnp.where(_nm, 1.0, 0.0).astype(jnp.float32)
        return (x, adj, nodemask)
    x, adj, nodemask = _rec_inputs()

    def _L0_gnn_setup():
        import jax, jax.numpy as jnp
        import numpy as np
        B, N, D = (2, 2048, 128)
        key = jax.random.key(seed)
        ks = jax.random.split(key, 6)
        return {'hidden': jax.random.normal(ks[0], (B, N, D), dtype=jnp.float32), 'mask': jax.random.uniform(ks[1], (B, N, N), dtype=jnp.float32), 'W_w': jax.random.normal(ks[2], (D, D), dtype=jnp.float32) * 0.05, 'W_b': jax.random.normal(ks[3], (D,), dtype=jnp.float32) * 0.05, 'a_w': jax.random.normal(ks[4], (2 * D,), dtype=jnp.float32) * 0.05, 'a_b': jax.random.normal(ks[5], (1,), dtype=jnp.float32) * 0.05}
    _L0_gnn_all = _L0_gnn_setup()
    _L0_gnn_in = {k: v for k, v in _L0_gnn_all.items() if k in ('W_w', 'W_b', 'a_w', 'a_b')}
    del _L0_gnn_all

    def _L1_gnn_setup():
        import jax, jax.numpy as jnp
        import numpy as np
        B, N, D, C, L = (64, 256, 128, 128, 5)
        EDGE_P = 0.02

        def _gru_cell(m, h, w_ih, w_hh, b_ih, b_hh):
            gi = m @ w_ih.T + b_ih
            gh = h @ w_hh.T + b_hh
            i_r, i_z, i_n = jnp.split(gi, 3, axis=-1)
            h_r, h_z, h_n = jnp.split(gh, 3, axis=-1)
            r = jax.nn.sigmoid(i_r + h_r)
            z = jax.nn.sigmoid(i_z + h_z)
            n = jnp.tanh(i_n + r * h_n)
            return (1.0 - z) * n + z * h
        key = jax.random.key(seed)
        ks = jax.random.split(key, 8)
        x = jax.random.normal(ks[0], (B, N, D), dtype=jnp.float32)
        adj = (jax.random.uniform(ks[1], (B, N, N)) < EDGE_P).astype(jnp.float32)
        mask = jnp.ones((B, N), dtype=jnp.float32)
        s = 1.0 / np.sqrt(C).astype(np.float32)
        weight = jax.random.uniform(ks[2], (L, C, C), minval=-s, maxval=s, dtype=jnp.float32)
        w_ih = jax.random.uniform(ks[3], (3 * C, C), minval=-s, maxval=s, dtype=jnp.float32)
        w_hh = jax.random.uniform(ks[4], (3 * C, C), minval=-s, maxval=s, dtype=jnp.float32)
        b_ih = jax.random.uniform(ks[5], (3 * C,), minval=-s, maxval=s, dtype=jnp.float32)
        b_hh = jax.random.uniform(ks[6], (3 * C,), minval=-s, maxval=s, dtype=jnp.float32)
        return dict(x=x, adj=adj, mask=mask, weight=weight, w_ih=w_ih, w_hh=w_hh, b_ih=b_ih, b_hh=b_hh)
    _L1_gnn_all = _L1_gnn_setup()
    _L1_gnn_in = {k: v for k, v in _L1_gnn_all.items() if k in ('weight', 'w_ih', 'w_hh', 'b_ih', 'b_hh')}
    del _L1_gnn_all

    def _L2_gnn_setup():
        import jax, jax.numpy as jnp
        import numpy as np
        IN_DIM = 128
        OUT_DIM = 128
        key = jax.random.key(seed)
        k1, k2, k3, k4 = jax.random.split(key, 4)
        B, N = (8, 1024)
        X = jax.random.normal(k1, (B, N, IN_DIM), dtype=jnp.float32)
        adj = jax.random.uniform(k2, (B, N, N), dtype=jnp.float32)
        bound = 1.0 / np.sqrt(IN_DIM)
        W = jax.random.uniform(k3, (OUT_DIM, IN_DIM), minval=-bound, maxval=bound, dtype=jnp.float32)
        b = jax.random.uniform(k4, (OUT_DIM,), minval=-bound, maxval=bound, dtype=jnp.float32)
        return {'X': X, 'adj': adj, 'W': W, 'b': b}
    _L2_gnn_all = _L2_gnn_setup()
    _L2_gnn_in = {k: v for k, v in _L2_gnn_all.items() if k in ('W', 'b')}
    del _L2_gnn_all

    def _L3_gnn_setup():
        import jax, jax.numpy as jnp
        import numpy as np
        DIM = 128
        HEADS = 8
        BS = 8
        N = 512
        NEG = -1000000000.0
        key = jax.random.key(seed)
        ks = jax.random.split(key, 8)
        feats = jax.random.normal(ks[0], (BS, N, DIM), dtype=jnp.float32)
        adj_mat = (jax.random.uniform(ks[1], (BS, N, N)) < 0.1).astype(jnp.float32)
        s = 1.0 / np.sqrt(DIM)
        fc_w = jax.random.normal(ks[2], (DIM, DIM * HEADS), dtype=jnp.float32) * s
        fc_b = jnp.zeros((DIM * HEADS,), dtype=jnp.float32)
        q_w = jax.random.normal(ks[3], (DIM, 1), dtype=jnp.float32) * s
        q_b = jnp.zeros((1,), dtype=jnp.float32)
        k_w = jax.random.normal(ks[4], (DIM, 1), dtype=jnp.float32) * s
        k_b = jnp.zeros((1,), dtype=jnp.float32)
        fp_w = jax.random.normal(ks[5], (DIM * HEADS, DIM), dtype=jnp.float32) * (1.0 / np.sqrt(DIM * HEADS))
        fp_b = jnp.zeros((DIM,), dtype=jnp.float32)
        return {'feats': feats, 'adj_mat': adj_mat, 'fc_w': fc_w, 'fc_b': fc_b, 'q_w': q_w, 'q_b': q_b, 'k_w': k_w, 'k_b': k_b, 'fp_w': fp_w, 'fp_b': fp_b}
    _L3_gnn_all = _L3_gnn_setup()
    _L3_gnn_in = {k: v for k, v in _L3_gnn_all.items() if k in ('fc_w', 'fc_b', 'q_w', 'q_b', 'k_w', 'k_b', 'fp_w', 'fp_b')}
    del _L3_gnn_all
    return {'x': x, 'adj': adj, 'nodemask': nodemask, 'L0_gnn_W_w': _L0_gnn_in['W_w'], 'L0_gnn_W_b': _L0_gnn_in['W_b'], 'L0_gnn_a_w': _L0_gnn_in['a_w'], 'L0_gnn_a_b': _L0_gnn_in['a_b'], 'L1_gnn_weight': _L1_gnn_in['weight'], 'L1_gnn_w_ih': _L1_gnn_in['w_ih'], 'L1_gnn_w_hh': _L1_gnn_in['w_hh'], 'L1_gnn_b_ih': _L1_gnn_in['b_ih'], 'L1_gnn_b_hh': _L1_gnn_in['b_hh'], 'L2_gnn_W': _L2_gnn_in['W'], 'L2_gnn_b': _L2_gnn_in['b'], 'L3_gnn_fc_w': _L3_gnn_in['fc_w'], 'L3_gnn_fc_b': _L3_gnn_in['fc_b'], 'L3_gnn_q_w': _L3_gnn_in['q_w'], 'L3_gnn_q_b': _L3_gnn_in['q_b'], 'L3_gnn_k_w': _L3_gnn_in['k_w'], 'L3_gnn_k_b': _L3_gnn_in['k_b'], 'L3_gnn_fp_w': _L3_gnn_in['fp_w'], 'L3_gnn_fp_b': _L3_gnn_in['fp_b']}

def reference(x, adj, nodemask, L0_gnn_W_w, L0_gnn_W_b, L0_gnn_a_w, L0_gnn_a_b, L1_gnn_weight, L1_gnn_w_ih, L1_gnn_w_hh, L1_gnn_b_ih, L1_gnn_b_hh, L2_gnn_W, L2_gnn_b, L3_gnn_fc_w, L3_gnn_fc_b, L3_gnn_q_w, L3_gnn_q_b, L3_gnn_k_w, L3_gnn_k_b, L3_gnn_fp_w, L3_gnn_fp_b):
    import jax
    import jax.numpy as jnp

    def _L0_gnn_ref(hidden, mask, W_w, W_b, a_w, a_b):
        import jax, jax.numpy as jnp
        import numpy as np
        B, N, D = (2, 2048, 128)
        h = jnp.einsum('bnd,ed->bne', hidden, W_w) + W_b
        Dh = h.shape[-1]
        a1, a2 = (a_w[:Dh], a_w[Dh:])
        e = h @ a1
        f = h @ a2
        logits = e[:, :, None] + f[:, None, :] + a_b[0]
        u = mask * jnp.exp(logits)
        a = u / jnp.sum(u, axis=2, keepdims=True)
        h_prime = jnp.einsum('bnm,bmd->bnd', a, h)
        return h_prime

    def _L1_gnn_ref(x, adj, mask, weight, w_ih, w_hh, b_ih, b_hh):
        import jax, jax.numpy as jnp
        import numpy as np
        B, N, D, C, L = (64, 256, 128, 128, 5)
        EDGE_P = 0.02

        def _gru_cell(m, h, w_ih, w_hh, b_ih, b_hh):
            gi = m @ w_ih.T + b_ih
            gh = h @ w_hh.T + b_hh
            i_r, i_z, i_n = jnp.split(gi, 3, axis=-1)
            h_r, h_z, h_n = jnp.split(gh, 3, axis=-1)
            r = jax.nn.sigmoid(i_r + h_r)
            z = jax.nn.sigmoid(i_z + h_z)
            n = jnp.tanh(i_n + r * h_n)
            return (1.0 - z) * n + z * h
        A = (adj != 0).astype(x.dtype)
        h = x
        for l in range(weight.shape[0]):
            m = jnp.einsum('bnd,de->bne', h, weight[l])
            agg = jnp.einsum('bij,bid->bjd', A, m)
            h = _gru_cell(agg, h, w_ih, w_hh, b_ih, b_hh)
        return h * mask[..., None]

    def _L2_gnn_ref(X, adj, W, b):
        import jax, jax.numpy as jnp
        import numpy as np
        IN_DIM = 128
        OUT_DIM = 128
        N = adj.shape[-1]
        adj_hat = adj + jnp.eye(N, dtype=adj.dtype)
        d = jnp.sum(adj_hat, axis=-1) ** (-0.5)
        adj_norm = d[..., :, None] * adj_hat * d[..., None, :]
        H = jnp.matmul(adj_norm, X)
        out = jnp.einsum('bnf,of->bno', H, W) + b
        return jax.nn.relu(out)

    def _L3_gnn_ref(feats, adj_mat, fc_w, fc_b, q_w, q_b, k_w, k_b, fp_w, fp_b):
        import jax, jax.numpy as jnp
        import numpy as np
        DIM = 128
        HEADS = 8
        BS = 8
        N = 512
        NEG = -1000000000.0
        bs, n, dim = feats.shape
        feat_proj = (feats @ fc_w + fc_b).reshape(bs, n, HEADS, dim).transpose(0, 2, 1, 3)
        q = feat_proj @ q_w + q_b
        k = feat_proj @ k_w + k_b
        logits = q + jnp.swapaxes(k, -1, -2)
        masked = logits + (1.0 - adj_mat[:, None]) * NEG
        masked = jax.nn.leaky_relu(masked, negative_slope=0.01)
        attn = jax.nn.softmax(masked, axis=-1)
        out = attn @ feat_proj
        out = out.transpose(0, 2, 1, 3).reshape(bs, n, HEADS * dim)
        out = out @ fp_w + fp_b + feats
        return jax.nn.sigmoid(out)
    h = jnp.maximum(_layernorm(x, axis=-1), 0.0)
    x = x + _L0_gnn_ref(h, adj, L0_gnn_W_w, L0_gnn_W_b, L0_gnn_a_w, L0_gnn_a_b)
    h = jnp.maximum(_layernorm(x, axis=-1), 0.0)
    x = x + _L1_gnn_ref(h, adj, nodemask, L1_gnn_weight, L1_gnn_w_ih, L1_gnn_w_hh, L1_gnn_b_ih, L1_gnn_b_hh)
    h = jnp.maximum(_layernorm(x, axis=-1), 0.0)
    x = x + _L2_gnn_ref(h, adj, L2_gnn_W, L2_gnn_b)
    h = jnp.maximum(_layernorm(x, axis=-1), 0.0)
    x = x + _L3_gnn_ref(h, adj, L3_gnn_fc_w, L3_gnn_fc_b, L3_gnn_q_w, L3_gnn_q_b, L3_gnn_k_w, L3_gnn_k_b, L3_gnn_fp_w, L3_gnn_fp_b)
    return x

_drawn_inputs = setup_inputs


def setup_inputs(seed=0):
    import zlib

    import numpy as np

    out = dict(_drawn_inputs(seed))
    spreads = {'L3_gnn_fc_b': (0.0, 0.563), 'L3_gnn_fp_b': (0.0, 0.551)}
    factors = {'L0_gnn_a_w': 2.703}
    for name, (base, spread) in spreads.items():
        noise = np.random.default_rng([zlib.crc32(name.encode()), seed]).standard_normal(out[name].shape)
        drawn = base * np.exp(spread * noise) if base else spread * noise
        out[name] = jnp.asarray(drawn.astype(out[name].dtype))
    for name, factor in factors.items():
        out[name] = (out[name] * factor).astype(out[name].dtype)
    return out
```

```python
from contextlib import ExitStack

import concourse.bass as bass
from concourse import mybir

F32 = mybir.dt.float32
F32R = mybir.dt.float32r
ALU = mybir.AluOpType
ACT = mybir.ActivationFunctionType
AX = mybir.AxisListType

P = 128
GRAPHS = 64
GW = 4
NG = GRAPHS // GW
HEADS = 8
STEPS = 5
EPS = 1e-5
NEG = -1e9
SLOPE = 0.01
ROWS = GW * P
LOW = 32
A_PH, B_PH, D_PH, E_PH = range(4)


def back(eng, sem, value):
    if isinstance(value, int) and value <= 0:
        return
    eng.wait_ge(sem, value)


def alone(eng, met):
    eng.sem_inc(met, 1)


def sweep(eng, stages, blocks=1, n=NG):
    lead = max(o for o, _ in stages)
    lag = -min(o for o, _ in stages)
    first = 2 + lag + (lag % 2)
    last = n - lead - (lead % 2)

    def written_out(i):
        for o, stage in stages:
            t = i + o
            if 0 <= t < n * blocks:
                stage(t % n, t % 2, t // n)

    for i in range(-lead, 0):
        written_out(i)
    for block in range(blocks):
        for g in range(0, first):
            written_out(block * n + g)
        with eng.Fori(first // 2, last // 2) as pair:
            for parity in range(2):
                for o, stage in stages:
                    stage(pair * 2 + (parity + o), (parity + o) % 2, block)
        for g in range(last, n):
            written_out(block * n + g)
    for i in range(n * blocks, n * blocks + lag):
        written_out(i)


def build(nc, x_in, adj_in, mask_in, w0_in, b0_in, a_in, ab_in, gw_in, wih_in, whh_in, bih_in, bhh_in,
          w2_in, b2_in, fc_in, fcb_in, qw_in, qb_in, kw_in, kb_in, fp_in, fpb_in, out, upto=4):
    with ExitStack() as ctx:
        def sb(name, shape, dt=F32):
            return ctx.enter_context(nc.sbuf_tensor(name, shape, dt))

        def sem(name):
            return ctx.enter_context(nc.semaphore(name))

        x_all = sb("x_all", [P, NG, GW, P])
        ident = sb("ident", [P, P])
        half = sb("half", [P, GW])
        edges = sb("edges", [P, NG, GW, P])
        hT_all = sb("hT_all", [P, NG, ROWS])
        gT_all = sb("gT_all", [P, NG, ROWS])
        W0e = sb("W0e", [P, P + 2])
        c0 = sb("c0", [P, 2])
        b0row = sb("b0row", [P, P])
        ab = sb("ab", [P, 1])
        gru_w = sb("gru_w", [P, 2, STEPS + 1, 3 * P], F32R)
        gate_b = sb("gate_b", [P, 4])
        maskT = sb("maskT", [P, GRAPHS])
        W2T = sb("W2T", [P, P])
        b2row = sb("b2row", [P, P])
        deg = sb("deg", [P, NG, GW])
        G = sb("G", [P, 2, HEADS * P], F32R)
        Wk = sb("Wk", [P, LOW + HEADS])
        Wq = sb("Wq", [P, GW, 2 * LOW])
        ck = sb("ck", [P, 1])
        cq = sb("cq", [P, 1])
        ce = sb("ce", [P, P])
        selk = sb("selk", [LOW + HEADS, HEADS, P], F32R)
        bn = sb("bn", [P, 2, GW, 6])
        mv = sb("mv", [P, 2, GW, 2])
        ve = sb("ve", [P, 2, GW])
        rstd = sb("rstd", [P, 2, GW])
        nmr = sb("nmr", [P, 2, GW])
        w1 = [sb(f"work{i}", [P, 2, GW, P]) for i in range(7)]
        split = sb("split", [P, 2, 4, ROWS], F32R)
        small = sb("small", [P, 2, 8, GW])
        ps = ctx.enter_context(nc.psum_tensor("ps", [P, 8, 512], F32))

        st = hT_all[:, :, :].rearrange("p a b -> p (a b)")
        sT = gT_all[:, :, :].rearrange("p a b -> p (a b)")
        r_w0, r_w2, r_mask = st[:, 0:128], st[:, 128:256], st[0:GRAPHS, 256:384]
        r_gw = st[:, 384:1024].rearrange("p (l e) -> p l e", e=P)
        r_wih = st[:, 1024:1408].rearrange("p (l e) -> p l e", e=P)
        r_whh = st[:, 1408:1792].rearrange("p (l e) -> p l e", e=P)
        r_fc = st[:, 1792:2816].rearrange("p (l e) -> p l e", e=P)
        r_fp = st[:, 6272:7296].rearrange("p (l e) -> p l e", e=P)
        r_vec = st[0:19, 3712:3840]
        vec0 = (9 + STEPS + HEADS) * P
        r_a, r_b0 = sT[:, vec0:vec0 + 2], sT[:, vec0 + 2:vec0 + 3]
        r_bih, r_bhh = sT[:, vec0 + 3:vec0 + 6], sT[:, vec0 + 6:vec0 + 9]
        r_fcb, r_qk = sT[:, vec0 + 9:vec0 + 17], sT[:, vec0 + 17:vec0 + 19]
        r_qb, r_kb = st[:, 3859:3860], st[:, 3860:3861]
        b0rep = st[:, 3968:4096]
        fcbk = st[:, 4096:4096 + 64]
        fcbq = st[:, 4160:4160 + 64]
        fcbrep = st[:, 4224:4224 + 1024].rearrange("p (h e) -> p h e", e=P)
        tiles = [r_w0, r_w2, r_mask, r_whh[:, 0], r_whh[:, 1], r_whh[:, 2], r_wih[:, 0], r_wih[:, 1], r_wih[:, 2]]
        tiles += [r_gw[:, l] for l in range(STEPS)] + [r_fc[:, h] for h in range(HEADS)] + [r_vec]
        T_W0, T_W2, T_MASK, T_WHH, T_WIH, T_GW, T_FC = 0, 1, 2, 3, 6, 9, 9 + STEPS
        NT = len(tiles)
        TB = -(-NT // 4)
        assert TB <= 6

        w_in, p_id0, p_id = sem("weights_in"), sem("prep_ident_zero"), sem("prep_ident")
        p_T, p_Tc, p_bld = sem("prep_transposed"), sem("prep_transposes_kept"), sem("prep_built")
        p_mm, p_hi, p_done = sem("prep_products"), sem("prep_high"), sem("prep_done")
        p_zero = sem("prep_zeroed")
        p_ahi = sem("prep_act_high")
        dve_met, pool_met = sem("vector_waits_met"), sem("gpsimd_waits_met")
        ln_bn, ln_mv, ln_ve = sem("ln_bn"), sem("ln_mv"), sem("ln_ve")
        ln_rstd, ln_nmr, ln_h = sem("ln_rstd"), sem("ln_nmr"), sem("ln_h")
        x_ld = [sem(f"x_landed{i}") for i in range(2)]
        a_ld = [sem(f"adj_landed{i}") for i in range(2)]
        a_T, a_adjT, a_hT = sem("a_transposed"), sem("a_adjT_kept"), sem("a_hT_kept")
        a_proj, a_exp, a_Y, a_agg = sem("a_projected"), sem("a_exps"), sem("a_Y"), sem("a_aggregated")
        a_edges, a_xb, a_s1, a_s2, a_s3 = sem("a_edges"), sem("a_xb"), sem("a_den"), sem("a_rden"), sem("a_scale")
        a_x1 = sem("a_x1")
        a_ycol = sem("a_ycol")
        b_T, b_hT, b_g, b_gT = sem("b_transposed"), sem("b_hT_kept"), sem("b_aggregated"), sem("b_gT_kept")
        c_hhi, c_hsp, c_ghi, c_glo = sem("c_h_high"), sem("c_h_split"), sem("c_g_high"), sem("c_g_low")
        c_r, c_hn, c_in, c_z = sem("c_r_ready"), sem("c_hn_ready"), sem("c_in_ready"), sem("c_z_ready")
        c_sr, c_sz, c_t1, c_t2, c_n = sem("c_r"), sem("c_z"), sem("c_t1"), sem("c_t2"), sem("c_n")
        c_d, c_zd, c_h = sem("c_h_minus_n"), sem("c_z_times"), sem("c_h_new")
        c_hk, c_T, c_nat, c_g, c_gk = sem("c_h_kept"), sem("c_transposed"), sem("c_nat"), sem("c_aggregated"), sem("c_g_kept")
        c_x2 = sem("c_x2")
        d_ld = [sem(f"d_adj_landed{i}") for i in range(2)]
        d_pow, d_dscale, d_T, d_adjT = sem("d_pow"), sem("d_scale"), sem("d_transposed"), sem("d_adjT")
        d_HT, d_HTk, d_o, d_t, d_t1, d_x3 = (sem("d_HT"), sem("d_HT_kept"), sem("d_out"), sem("d_scaled"),
                                             sem("d_biased"), sem("d_x3"))
        e_ld = [sem(f"e_adj_landed{i}") for i in range(2)]
        e_qsel = sem("e_qsel")
        e_T, e_hT, e_hhi, e_split = sem("e_transposed"), sem("e_hT_kept"), sem("e_h_high"), sem("e_h_split")
        e_k, e_kb, e_khi, e_K = sem("e_k"), sem("e_k_biased"), sem("e_k_high"), sem("e_K_rows")
        e_q, e_qb, e_qhi, e_Q = sem("e_q"), sem("e_q_biased"), sem("e_q_high"), sem("e_Q_rows")
        e_V, e_Vk, e_M, e_hc = sem("e_V"), sem("e_V_kept"), sem("e_M"), sem("e_hc")
        e_o, e_th, e_sg, e_x4 = sem("e_o"), sem("e_tanh"), sem("e_sigmoid"), sem("e_x4")
        u_S, u_X, u_mx, u_Y, u_Z, u_E = sem("u_S"), sem("u_X"), sem("u_max"), sem("u_leaky"), sem("u_shifted"), sem("u_exp")
        u_s, u_r, u_P, u_T, u_A, u_AV = sem("u_sum"), sem("u_rsum"), sem("u_probs"), sem("u_T"), sem("u_A_kept"), sem("u_AV")
        o_st = sem("out_stored")

        block = ctx.enter_context(nc.Block())

        def bcast(ap, n=GW):
            return ap.unsqueeze(1).to_broadcast([ap.shape[0], n, ap.shape[1]])

        def along(ap, n=P):
            return ap.unsqueeze(2).to_broadcast([ap.shape[0], ap.shape[1], n])

        WLOADS = [
            (r_w0, w0_in), (r_w2, w2_in), (r_mask, mask_in),
            (r_whh, whh_in.rearrange("(k r) d -> r k d", r=P)), (r_wih, wih_in.rearrange("(k r) d -> r k d", r=P)),
            (r_gw, gw_in.rearrange("l d e -> d l e")), (r_fc, fc_in.rearrange("d (h e) -> d h e", e=P)),
            (r_fp, fp_in.rearrange("(h c) e -> c h e", c=P)),
            (r_vec[0:2], a_in.rearrange("(t e) -> t e", e=P)), (r_vec[2:3], b0_in.rearrange("(t e) -> t e", e=P)),
            (r_vec[3:6], bih_in.rearrange("(t e) -> t e", e=P)), (r_vec[6:9], bhh_in.rearrange("(t e) -> t e", e=P)),
            (r_vec[9:17], fcb_in.rearrange("(t e) -> t e", e=P)), (r_vec[17:18], qw_in.rearrange("e t -> t e")),
            (r_vec[18:19], kw_in.rearrange("e t -> t e")),
            (r_qb, qb_in.partition_broadcast(P)), (r_kb, kb_in.partition_broadcast(P)),
            (ab[:, :], ab_in.partition_broadcast(P)), (b0row[:, :], b0_in.partition_broadcast(P)),
            (b2row[:, :], b2_in.partition_broadcast(P)), (ce[:, :], fpb_in.partition_broadcast(P)),
        ]

        x_dram = x_in.rearrange("(g j) n d -> n g j d", j=GW)
        adj_dram = adj_in.rearrange("(g j) n m -> n g j m", j=GW)
        out_dram = out.rearrange("(g j) n d -> n g j d", j=GW)
        adj_s, h_s, hT_s, adjT_s, xb_s = w1[0], w1[1], w1[2], w1[3], w1[4]
        Y_s = [w1[5][:, :, :, :].rearrange("p b j e -> p (b j e)")[:, 0:GW * (P + 2)].rearrange("p (j e) -> p j e", e=P + 2),
               w1[6][:, :, :, :].rearrange("p b j e -> p (b j e)")[:, 0:GW * (P + 2)].rearrange("p (j e) -> p j e", e=P + 2)]

        qsel = gru_w[:, :, :, :].rearrange("p a w c -> p (a w c)")[0:2 * LOW, 0:HEADS * ROWS]
        V = st.rearrange("p (b j c) -> p b j c", b=2, j=GW)
        unit = edges[:, :, :, :].rearrange("p (k b) j e -> p k b j e", b=2)
        X_u, Y_u, Z_u, E_u, P_u, A_u = (unit[:, k] for k in range(6))
        he_s, heT_s, M_s, kf_s = w1[1], w1[2], w1[3], w1[4]
        spare = gT_all[:, :, :].rearrange("p (k b) r -> p k b r", b=2)
        hc_s, o_s, t_s, g_s, qf_s = (spare[:, k] for k in range(5))
        sm = small

        def flat(ap):
            return ap.rearrange("p j e -> p (j e)")

        def units(g, b, h, stages):
            for lag, stage in stages:
                if lag > h:
                    if not (isinstance(g, int) and g <= 0):
                        stage(g - 1, 1 - b, h - lag + HEADS)
                elif not (isinstance(g, int) and not 0 <= g < NG):
                    stage(g, b, h - lag)

        def has(g):
            return not isinstance(g, int) or 0 <= g < NG

        def value_chunk(g, b, h, stage):
            if h >= HEADS // 2:
                g, b, c = g + 1, 1 - b, h - HEADS // 2
            else:
                c = h + HEADS // 2
            if has(g):
                stage(g, b, c)

        def all_groups(eng, group):
            for g in range(-2, 4):
                group(g, g % 2)
            with eng.Fori(2, NG // 2 - 1) as pair:
                for b in range(2):
                    group(pair * 2 + b, b)
            for g in (NG - 2, NG - 1, NG):
                group(g, g % 2)

        @block.sync
        def _(sp):
            for dst, src in WLOADS[:11]:
                sp.dma_start(dst, src).then_inc(w_in, 16)

            def load_x(g, b, _):
                back(sp, x_ld[b], (g - b) * 8)
                sp.dma_start(x_all[:, g], x_dram[:, g]).then_inc(x_ld[b], 16)

            def load_adj(g, b, _):
                back(sp, a_edges, g - 1)
                back(sp, a_T, g - 1)
                sp.dma_start(adj_s[:, b], adj_dram[:, g]).then_inc(a_ld[b], 16)

            sweep(sp, [(0, load_x), (0, load_adj)])

            if upto >= 3:
                sp.wait_ge(c_x2, NG)

                def load_adj2(g, b, _):
                    back(sp, d_T, g - 1)
                    sp.dma_start(adj_s[:, b], adj_dram[:, g]).then_inc(d_ld[b], 16)

                sweep(sp, [(0, load_adj2)])

            if upto >= 4:
                sp.wait_ge(d_T, NG)

                def load_adj3(g, b, _):
                    back(sp, e_M, g - 1)
                    sp.dma_start(adj_s[:, b], adj_dram[:, g]).then_inc(e_ld[b], 16)
                    if isinstance(g, int) and g < 2:
                        return
                    sp.wait_ge(e_x4, g - 1)
                    sp.dma_start(out_dram[:, g - 2], x_all[:, g - 2]).then_inc(o_st, 16)

                sweep(sp, [(0, load_adj3)])
                for g in (NG - 2, NG - 1):
                    sp.wait_ge(e_x4, g + 1)
                    sp.dma_start(out_dram[:, g], x_all[:, g]).then_inc(o_st, 16)
                sp.wait_ge(o_st, 16 * NG)
                return

            final = {1: a_x1, 2: c_x2, 3: d_x3, 4: e_x4}[upto]

            def store(g, b, _):
                sp.wait_ge(final, g + 1)
                sp.dma_start(out_dram[:, g], x_all[:, g]).then_inc(o_st, 16)

            sweep(sp, [(0, store)])
            sp.wait_ge(o_st, 16 * NG)

        @block.gpsimd
        def _(pool):
            pool.memset(ident[:, :], 0.0).then_inc(p_id0, 1)
            pool.memset(half[:, :], -0.5)
            pool.memset(fcbk, 0.0)
            pool.memset(Wk[:, :], 0.0)
            pool.memset(Wq[:, :, :], 0.0).then_inc(p_id0, 1)
            pool.wait_ge(p_id0, 2)
            pool.affine_select(out=ident[:, :], in_=ident[:, :], compare_op=ALU.not_equal, fill=1.0, base=0,
                               pattern=[[-1, P]], channel_multiplier=1).then_inc(p_id, 1)

            def ln_pow(ph):
                def stage(g, b, _):
                    t = g + NG * ph
                    pool.wait_ge(ln_ve, t + 1)
                    back(pool, ln_h, t - 1)
                    pool.tensor_tensor(rstd[:, b], ve[:, b], half[:, :], ALU.pow).then_inc(ln_rstd, 1)
                return stage

            def x_plus_b(g, b, _):
                pool.wait_ge(w_in, 16 * len(WLOADS))
                pool.wait_ge(x_ld[b], (g - b) * 8 + 16)
                back(pool, a_x1, g - 1)
                pool.tensor_tensor(xb_s[:, b], x_all[:, g], bcast(b0row[:, :]), ALU.add).then_inc(a_xb, 1)

            sweep(pool, [(0, ln_pow(A_PH)), (0, x_plus_b)])
            if upto < 2:
                return
            sweep(pool, [(0, ln_pow(B_PH))])

            def h_minus_n(g, b, l):
                t = g + NG * l
                pool.wait_ge(c_n, t + 1)
                back(pool, c_h, t - 1)
                pool.tensor_tensor(w1[4][:, b].rearrange("p j e -> p (j e)"), hT_all[:, g],
                                   w1[3][:, b].rearrange("p j e -> p (j e)"), ALU.subtract).then_inc(c_d, 1)
                pool.wait_ge(c_d, t + 1)
                pool.wait_ge(c_sz, t + 1)
                pool.tensor_tensor(w1[4][:, b], w1[4][:, b], w1[1][:, b], ALU.mult).then_inc(c_zd, 1)

            sweep(pool, [(0, h_minus_n)], STEPS)
            if upto < 3:
                return
            pool.wait_ge(a_s3, 2 * NG)
            for g in range(0, NG):
                pool.tensor_tensor(deg[:, g], deg[:, g], half[:, :], ALU.pow).then_inc(d_pow, 1)
            sweep(pool, [(0, ln_pow(D_PH))])
            if upto < 4:
                return

            def shift(g, b, h):
                u = g * HEADS + h
                q = h % 2
                pool.wait_ge(u_Y, u + 1)
                pool.wait_ge(u_mx, u + 1)
                back(pool, u_E, u - 1)
                pool.tensor_tensor(Z_u[:, q], Y_u[:, q], along(sm[:, q, 1]), ALU.subtract).then_inc(u_Z, 1)

            def normalize(g, b, h):
                u = g * HEADS + h
                q = h % 2
                pool.wait_ge(u_r, u + 1)
                back(pool, u_T, u - 1)
                pool.tensor_tensor(P_u[:, q], E_u[:, q], along(sm[:, q, 3]), ALU.mult).then_inc(u_P, 1)

            def sigmoid(g, b, h):
                if h == HEADS - 1:
                    pool.wait_ge(e_th, g + 1)
                    back(pool, e_x4, g - 1)
                    alone(pool, pool_met)
                    pool.tensor_scalar(g_s[:, b], t_s[:, b], 0.5, 0.5, ALU.mult, ALU.add).then_inc(e_sg, 1)

            ln_pow_e = ln_pow(E_PH)

            def group(g, b):
                for h in range(HEADS):
                    units(g, b, h, [(0, shift), (2, normalize), (6, sigmoid)])
                    if h == 2 and has(g + 2):
                        ln_pow_e(g + 2, b, 0)
                    if h == 5 and has(g + 1):
                        pool.wait_ge(ln_h, NG * E_PH + (g + 1) + 1)
                        back(pool, e_o, g)
                        pool.tensor_tensor(hc_s[:, 1 - b].rearrange("p (j e) -> p j e", e=P), he_s[:, 1 - b],
                                           bcast(ce[:, :]), ALU.add).then_inc(e_hc, 1)

            all_groups(pool, group)

        @block.vector
        def _(dve):
            def ln_stats(ph, ready):
                def stage(g, b, _):
                    t = g + NG * ph
                    ready(g, b)
                    for j in range(GW):
                        last = dve.bn_stats(bn[:, b, j], x_all[:, g, j])
                    last.then_inc(ln_bn, 1)
                    dve.wait_ge(ln_bn, t + 1)
                    back(dve, ln_nmr, t - 1)
                    alone(dve, dve_met)
                    for j in range(GW):
                        last = dve.bn_aggr(mv[:, b, j], bn[:, b, j])
                    last.then_inc(ln_mv, 1)
                    dve.wait_ge(ln_mv, t + 1)
                    back(dve, ln_rstd, t - 1)
                    dve.tensor_scalar(ve[:, b], mv[:, b, :, 1], EPS, None, ALU.add).then_inc(ln_ve, 1)
                return stage

            def ln_shift(ph, gcn=False):
                def stage(g, b, _):
                    t = g + NG * ph
                    dve.wait_ge(ln_rstd, t + 1)
                    back(dve, ln_h, t - 1)
                    if gcn:
                        dve.tensor_tensor(small[:, b, 7], rstd[:, b], deg[:, g], ALU.mult).then_inc(d_dscale, 1)
                        dve.wait_ge(d_dscale, g + 1)
                        dve.scalar_tensor_tensor(nmr[:, b], mv[:, b, :, 0], -1.0, small[:, b, 7], ALU.mult,
                                                 ALU.mult).then_inc(ln_nmr, 1)
                    else:
                        dve.scalar_tensor_tensor(nmr[:, b], mv[:, b, :, 0], -1.0, rstd[:, b], ALU.mult,
                                                 ALU.mult).then_inc(ln_nmr, 1)
                return stage

            dve.wait_ge(w_in, 16 * len(WLOADS))
            dve.wait_ge(p_id0, 2)
            dve.wait_ge(p_id, 1)
            dve.tensor_copy(selk[0:LOW], along(ident[0:LOW, 0:HEADS]))
            dve.tensor_copy(selk[LOW:LOW + HEADS], along(ident[LOW:LOW + HEADS, LOW:LOW + HEADS]))
            for k in range(TB):
                n = min(4, NT - 4 * k) * P
                dve.wait_ge(p_T, k + 1)
                if k == 0:
                    dve.tensor_copy(sT[:, 0:256], ps[:, 0, 0:256])
                    dve.tensor_copy(maskT[:, :], ps[:, 0, 256:256 + GRAPHS])
                    dve.tensor_copy(sT[:, 384:512], ps[:, 0, 384:512]).then_inc(p_Tc, 1)
                elif k == TB - 1:
                    dve.tensor_copy(sT[:, 512 * k:vec0], ps[:, k, 0:vec0 - 512 * k])
                    dve.tensor_copy(sT[:, vec0:vec0 + 19], ps[:, k, vec0 - 512 * k:vec0 - 512 * k + 19]).then_inc(p_Tc, 1)
                else:
                    dve.tensor_copy(sT[:, 512 * k:512 * k + n], ps[:, k, 0:n]).then_inc(p_Tc, 1)
            dve.wait_ge(p_Tc, TB)
            dve.tensor_copy(b0rep, r_b0.to_broadcast([P, P]))
            dve.tensor_copy(fcbrep, along(r_fcb))
            dve.tensor_copy(fcbk[:, 0:HEADS], r_fcb)
            dve.tensor_copy(fcbk[:, LOW:LOW + HEADS], r_fcb)
            dve.tensor_copy(fcbq.rearrange("p (k h) -> p k h", h=HEADS), bcast(r_fcb, 8))
            dve.tensor_copy(gate_b[:, 2:3], r_bih[:, 2:3])
            dve.tensor_copy(gate_b[:, 3:4], r_bhh[:, 2:3])
            dve.tensor_tensor(gate_b[:, 0:2], r_bih[:, 0:2], r_bhh[:, 0:2], ALU.add).then_inc(p_bld, 1)
            dve.tensor_copy(W0e[:, 0:P], sT[:, 0:P])
            dve.tensor_copy(W2T[:, :], sT[:, P:2 * P])
            whhT = sT[:, T_WHH * P:(T_WHH + 3) * P]
            dve.tensor_copy(gru_w[:, 0, STEPS], whhT).then_inc(p_hi, 1)
            dve.wait_ge(p_hi, 1)
            dve.tensor_tensor(gru_w[:, 1, STEPS], whhT, gru_w[:, 0, STEPS].bitcast(F32), ALU.subtract)
            dve.wait_ge(p_mm, 1)
            dve.tensor_copy(W0e[:, P:P + 2], ps[:, 5, 0:2])
            dve.tensor_copy(c0[:, :], ps[:, 5, 2:4]).then_inc(p_hi, 1)
            dve.wait_ge(p_hi, 2)
            dve.tensor_tensor(c0[:, 0:1], c0[:, 0:1], ab[:, :], ALU.add)
            wqk = ps[:, 5, 8:8 + 2 * HEADS].rearrange("p (h t) -> p t h", t=2)
            dve.tensor_copy(Wk[:, 0:HEADS], wqk[:, 1])
            dve.tensor_copy(Wk[:, LOW:LOW + HEADS], wqk[:, 1])
            for j in range(GW):
                for k in range(2):
                    o = k * LOW + j * HEADS
                    dve.tensor_copy(Wq[:, j, o:o + HEADS], wqk[:, 0])
            dve.tensor_tensor(ck[0:LOW + HEADS], ps[0:LOW + HEADS, 5, 32:33], r_kb[0:LOW + HEADS], ALU.add)
            dve.tensor_tensor(cq[0:2 * LOW], ps[0:2 * LOW, 5, 33:34], r_qb[0:2 * LOW], ALU.add)
            dve.tensor_tensor(ce[:, :], ps[:, 5, 128:256], ce[:, :], ALU.add)
            for l in range(STEPS):
                dve.wait_ge(p_ahi, l + 1)
                dve.tensor_tensor(gru_w[:, 1, l], ps[:, l, 0:3 * P], gru_w[:, 0, l].bitcast(F32), ALU.subtract)
            for k in range(2):
                dve.wait_ge(p_ahi, STEPS + k + 1)
                s = slice(512 * k, 512 * k + 512)
                last = dve.tensor_tensor(G[:, 1, s], ps[:, 6 + k], G[:, 0, s].bitcast(F32), ALU.subtract)
            last.then_inc(p_done, 1)
            dve.wait_ge(p_done, 1)

            for b in range(2):
                last = dve.memset(Y_s[b][:, :, P + 1:P + 2], 1.0)
            last.then_inc(a_ycol, 1)

            def take_edges(g, b, _):
                dve.wait_ge(a_ld[b], (g - b) * 8 + 16)
                dve.tensor_scalar(edges[:, g], adj_s[:, b], 0.0, None, ALU.not_equal).then_inc(a_edges, 1)

            def scale_Y(g, b, _):
                dve.wait_ge(a_exp, 2 * g + 2)
                back(dve, a_agg, g - 1)
                for j in range(GW):
                    last = dve.tensor_scalar(Y_s[b][:, j, 0:P], ps[:, 2 + j // 2, (j % 2) * 256:(j % 2) * 256 + P],
                                             small[:, b, 1, j:j + 1], None, ALU.mult)
                dve.tensor_copy(Y_s[b][:, :, P], small[:, b, 1]).then_inc(a_Y, 1)

            def finish(g, b, _):
                dve.wait_ge(a_agg, g + 1)
                agg = ps[:, 4:6, :].rearrange("p k (j e) -> p k j e", e=256)
                den = small[:, b, 2].rearrange("p (k j) -> p k j", j=2)
                dve.tensor_copy(den, agg[:, :, :, P])
                dve.tensor_scalar(deg[:, g].rearrange("p (k j) -> p k j", j=2), agg[:, :, :, P + 1], 1.0, None,
                                  ALU.add).then_inc(a_s3, 1)
                dve.wait_ge(a_s3, 2 * g + 1)
                dve.tensor_tensor(small[:, b, 2], small[:, b, 2], small[:, b, 0], ALU.mult).then_inc(a_s1, 1)
                dve.wait_ge(a_s1, g + 1)
                dve.reciprocal(small[:, b, 3], small[:, b, 2]).then_inc(a_s2, 1)
                dve.wait_ge(a_s2, g + 1)
                dve.tensor_tensor(small[:, b, 4], small[:, b, 3], small[:, b, 0], ALU.mult).then_inc(a_s3, 1)
                dve.wait_ge(a_s3, 2 * g + 2)
                dve.wait_ge(a_xb, g + 1)
                for j in range(GW):
                    last = dve.scalar_tensor_tensor(x_all[:, g, j], ps[:, 4 + j // 2, (j % 2) * 256:(j % 2) * 256 + P],
                                                    small[:, b, 4, j:j + 1], xb_s[:, b, j], ALU.mult, ALU.add)
                last.then_inc(a_x1, 1)

            sweep(dve, [(2, ln_stats(A_PH, lambda g, b: dve.wait_ge(x_ld[b], (g - b) * 8 + 16))),
                        (1, ln_shift(A_PH)), (1, take_edges), (0, scale_Y), (-1, finish)])
            if upto < 2:
                return

            sweep(dve, [(2, ln_stats(B_PH, lambda g, b: dve.wait_ge(a_x1, g + 1))), (1, ln_shift(B_PH))])

            def split_hg(g, b, l):
                t = g + NG * l
                if l == 0:
                    dve.wait_ge(b_hT, g + 1)
                    dve.wait_ge(b_gT, g + 1)
                else:
                    dve.wait_ge(c_hk, t - NG + 1)
                    dve.wait_ge(c_gk, t - NG + 1)
                back(dve, c_z, t - 1)
                dve.tensor_copy(split[:, b, 0], hT_all[:, g]).then_inc(c_hhi, 1)
                dve.wait_ge(c_hhi, t + 1)
                dve.tensor_tensor(split[:, b, 1], hT_all[:, g], split[:, b, 0].bitcast(F32),
                                  ALU.subtract).then_inc(c_hsp, 1)
                dve.wait_ge(c_ghi, t + 1)
                dve.tensor_tensor(split[:, b, 3], gT_all[:, g], split[:, b, 2].bitcast(F32),
                                  ALU.subtract).then_inc(c_glo, 1)

            def new_state(g, b, l):
                t = g + NG * l
                dve.wait_ge(c_zd, t + 1)
                back(dve, c_T, t - 1)
                back(dve, c_hk, t - 1)
                dve.tensor_tensor(w1[5][:, b], w1[3][:, b], w1[4][:, b], ALU.add).then_inc(c_h, 1)
                if l == STEPS - 1:
                    pass

            def candidate(g, b, l):
                t = g + NG * l
                dve.wait_ge(c_sr, t + 1)
                dve.wait_ge(c_hn, t + 1)
                back(dve, c_n, t - 1)
                tt = w1[2][:, b].rearrange("p j e -> p (j e)")
                dve.scalar_tensor_tensor(tt, ps[:, 1], gate_b[:, 3:4], w1[0][:, b].rearrange("p j e -> p (j e)"),
                                         ALU.add, ALU.mult).then_inc(c_t1, 1)
                dve.wait_ge(c_t1, t + 1)
                dve.wait_ge(c_in, t + 1)
                dve.tensor_tensor(tt, ps[:, 2], tt, ALU.add).then_inc(c_t2, 1)

            def to_x(g, b, l):
                if l < STEPS - 1:
                    return
                t = g + NG * l
                dve.wait_ge(c_T, t + 1)
                for j in range(GW):
                    o = g * GW + j
                    m = maskT[:, bass.ds(o, 1)]
                    last = dve.scalar_tensor_tensor(x_all[:, g, j], ps[:, 4 + b, j * P:(j + 1) * P], m,
                                                    x_all[:, g, j], ALU.mult, ALU.add)
                last.then_inc(c_x2, 1)

            sweep(dve, [(1, split_hg), (-1, new_state), (0, candidate), (-2, to_x)], STEPS)
            if upto < 3:
                return

            dve.wait_ge(d_pow, NG)

            def add_self(g, b, _):
                dve.wait_ge(d_T, g + 1)
                back(dve, d_HT, g - 1)
                dve.tensor_tensor(adjT_s[:, b], ps[:, b].rearrange("p (j e) -> p j e", e=P), bcast(ident[:, :]),
                                  ALU.add).then_inc(d_adjT, 1)

            def finish2(g, b, _):
                dve.wait_ge(d_o, g + 1)
                for j in range(GW):
                    last = dve.scalar_tensor_tensor(w1[4][:, b, j], ps[:, 4 + b, j * P:(j + 1) * P], deg[:, g, j:j + 1],
                                                    b2row[:, :], ALU.mult, ALU.add)
                last.then_inc(d_t, 1)
                dve.wait_ge(d_t, g + 1)
                dve.scalar_tensor_tensor(x_all[:, g], w1[4][:, b], 0.0, x_all[:, g], ALU.max,
                                         ALU.add).then_inc(d_x3, 1)

            sweep(dve, [(2, ln_stats(D_PH - 0, lambda g, b: dve.wait_ge(c_x2, NG))), (1, ln_shift(D_PH, True)),
                        (0, add_self), (-1, finish2)])
            if upto < 4:
                return

            def mask_max(g, b, h):
                u = g * HEADS + h
                q = h % 2
                dve.wait_ge(u_S, u + 1)
                dve.wait_ge(e_M, g + 1)
                alone(dve, dve_met)
                for j in range(GW):
                    last = dve.tensor_tensor_reduce(X_u[:, q, j], ps[:, q, j * P:(j + 1) * P], M_s[:, b, j], 1.0, -3.0e38,
                                                    ALU.add, ALU.max, sm[:, q, 0, j:j + 1])
                last.then_inc(u_X, 1)
                dve.wait_ge(u_X, u + 1)
                back(dve, u_Z, u - 1)
                dve.scalar_tensor_tensor(sm[:, q, 1], sm[:, q, 0], SLOPE, sm[:, q, 0], ALU.mult,
                                         ALU.max).then_inc(u_mx, 1)
                dve.scalar_tensor_tensor(Y_u[:, q], X_u[:, q], SLOPE, X_u[:, q], ALU.mult,
                                         ALU.max).then_inc(u_Y, 1)

            def row_sums(g, b, h):
                u = g * HEADS + h
                q = h % 2
                dve.wait_ge(u_E, u + 1)
                back(dve, u_P, u - 1)
                dve.tensor_reduce(sm[:, q, 2], E_u[:, q], AX.X, ALU.add).then_inc(u_s, 1)
                dve.wait_ge(u_s, u + 1)
                dve.reciprocal(sm[:, q, 3], sm[:, q, 2]).then_inc(u_r, 1)

            def to_out(g, b, h):
                if h == HEADS - 1:
                    dve.wait_ge(u_AV, g * HEADS + HEADS)
                    dve.wait_ge(e_hc, g + 1)
                    back(dve, e_th, g - 1)
                    dve.tensor_tensor(o_s[:, b], ps[:, 4 + b], hc_s[:, b], ALU.add).then_inc(e_o, 1)

            def add_x(g, b, h):
                if h == HEADS - 1:
                    dve.wait_ge(e_sg, g + 1)
                    dve.tensor_tensor(x_all[:, g], g_s[:, b].rearrange("p (j e) -> p j e", e=P), x_all[:, g],
                                      ALU.add).then_inc(e_x4, 1)

            stats_e = ln_stats(E_PH, lambda g, b: dve.wait_ge(d_x3, g + 1))
            shift_e = ln_shift(E_PH)

            def split_rows(hi_sem, done, biased, rows_hi, rows_full, n, g):
                dve.wait_ge(biased, g + 1)
                dve.tensor_copy(rows_hi[0:n], rows_full[0:n]).then_inc(hi_sem, 1)
                dve.wait_ge(hi_sem, g + 1)
                dve.tensor_tensor(rows_hi[LOW:n], rows_full[LOW:n], rows_hi[LOW:n].bitcast(F32),
                                  ALU.subtract).then_inc(done, 1)

            def group(g, b):
                for h in range(HEADS):
                    units(g, b, h, [(0, mask_max), (2, row_sums), (5, to_out), (7, add_x)])
                    if h == 1 and has(g + 1):
                        back(dve, u_S, g * HEADS)
                        split_rows(e_khi, e_K, e_kb, split[:, 1 - b, 2], flat(kf_s[:, 1 - b]), LOW + HEADS, g + 1)
                        split_rows(e_qhi, e_Q, e_qb, split[:, 1 - b, 3, 0:P], qf_s[:, 1 - b, 0:P], 2 * LOW, g + 1)
                    if h == 1 and has(g + 2):
                        stats_e(g + 2, b, 0)
                    if h == 3 and has(g + 2):
                        shift_e(g + 2, b, 0)
                    if h == 4 and has(g + 1):
                        dve.wait_ge(e_ld[1 - b], (g + 1 - (1 - b)) * 8 + 16)
                        back(dve, u_X, g * HEADS)
                        dve.tensor_scalar(M_s[:, 1 - b], adj_s[:, 1 - b], 1.0, -NEG, ALU.subtract,
                                          ALU.mult).then_inc(e_M, 1)
                    if h == 6 and has(g + 2):
                        dve.wait_ge(e_hT, g + 3)
                        back(dve, e_V, HEADS * (g + 1))
                        dve.tensor_copy(split[:, b, 0], flat(heT_s[:, b])).then_inc(e_hhi, 1)
                        dve.wait_ge(e_hhi, g + 3)
                        dve.tensor_tensor(split[:, b, 1], flat(heT_s[:, b]), split[:, b, 0].bitcast(F32),
                                          ALU.subtract).then_inc(e_split, 1)

            all_groups(dve, group)

        @block.scalar
        def _(act):
            for dst, src in WLOADS[11:]:
                act.dma_start(dst, src).then_inc(w_in, 16)

            def ln_apply(ph, dst, free, scale=None):
                def stage(g, b, _):
                    t = g + NG * ph
                    act.wait_ge(ln_nmr, t + 1)
                    free(g, b)
                    s = rstd[:, b] if scale is None else small[:, b, 7]
                    for j in range(GW):
                        last = act.activation(dst[:, b, j], x_all[:, g, j], ACT.Relu, bias=nmr[:, b, j:j + 1],
                                              scale=s[:, j:j + 1])
                    last.then_inc(ln_h, 1)
                return stage

            act.wait_ge(p_mm, 2)
            for l in range(STEPS):
                act.activation(gru_w[:, 0, l], ps[:, l, 0:3 * P], ACT.Copy).then_inc(p_ahi, 1)
            for k in range(2):
                act.activation(G[:, 0, 512 * k:512 * k + 512], ps[:, 6 + k], ACT.Copy).then_inc(p_ahi, 1)

            def keep_T(g, b, _):
                act.wait_ge(a_T, g + 1)
                back(act, a_proj, g - 1)
                act.activation(hT_s[:, b], ps[:, 0].rearrange("p (j e) -> p j e", e=P), ACT.Copy).then_inc(a_hT, 1)
                back(act, a_agg, g - 1)
                act.activation(adjT_s[:, b], ps[:, 1].rearrange("p (j e) -> p j e", e=P), ACT.Copy).then_inc(a_adjT, 1)

            def exps(g, b, _):
                act.wait_ge(a_proj, g + 1)
                back(act, a_x1, g - 1)
                fe = ps[:, 2:4, :].rearrange("p k (j e) -> p k j e", e=256)
                for k, c in ((0, 0), (1, 1)):
                    act.activation(small[:, b, k].rearrange("p (k j) -> p k j", j=2), fe[:, :, :, P + k], ACT.Exp,
                                   bias=c0[:, c:c + 1]).then_inc(a_exp, 1)

            sweep(act, [(1, ln_apply(A_PH, h_s, lambda g, b: back(act, a_T, g - 1))), (1, keep_T), (0, exps)])
            if upto < 2:
                return

            act.wait_ge(a_agg, NG)

            def keep_hT(g, b, _):
                act.wait_ge(b_T, g + 1)
                act.activation(hT_all[:, g], ps[:, b], ACT.Copy).then_inc(b_hT, 1)

            def keep_gT(g, b, _):
                act.wait_ge(b_g, g + 1)
                act.activation(gT_all[:, g], ps[:, 6 + b], ACT.Copy).then_inc(b_gT, 1)

            sweep(act, [(1, ln_apply(B_PH, w1[6], lambda g, b: back(act, b_g, g - 1))), (0, keep_hT), (-1, keep_gT)])

            def high_g(g, b, l):
                t = g + NG * l
                if l == 0:
                    act.wait_ge(b_gT, g + 1)
                else:
                    act.wait_ge(c_gk, t - NG + 1)
                back(act, c_z, t - 1)
                act.activation(split[:, b, 2], gT_all[:, g], ACT.Copy).then_inc(c_ghi, 1)

            def gates(g, b, l):
                t = g + NG * l
                act.wait_ge(c_r, t + 1)
                back(act, c_t1, t - 1)
                act.activation(w1[0][:, b].rearrange("p j e -> p (j e)"), ps[:, 0], ACT.Sigmoid,
                               bias=gate_b[:, 0:1]).then_inc(c_sr, 1)
                act.wait_ge(c_z, t + 1)
                back(act, c_zd, t - 1)
                act.activation(w1[1][:, b].rearrange("p j e -> p (j e)"), ps[:, 3], ACT.Sigmoid,
                               bias=gate_b[:, 1:2]).then_inc(c_sz, 1)
                act.wait_ge(c_t2, t + 1)
                back(act, c_h, t - 1)
                act.activation(w1[3][:, b], w1[2][:, b], ACT.Tanh, bias=gate_b[:, 2:3]).then_inc(c_n, 1)

            def keep_h(g, b, l):
                t = g + NG * l
                act.wait_ge(c_h, t + 1)
                act.activation(hT_all[:, g], w1[5][:, b].rearrange("p j e -> p (j e)"), ACT.Copy).then_inc(c_hk, 1)
                if l < STEPS - 1:
                    act.wait_ge(c_T, t + 1)
                    back(act, c_g, t - 1)
                    act.activation(w1[6][:, b].rearrange("p j e -> p (j e)"), ps[:, 4 + b], ACT.Copy).then_inc(c_nat, 1)

            def keep_g(g, b, l):
                if l == STEPS - 1:
                    return
                t = g + NG * l
                act.wait_ge(c_g, t + 1)
                act.activation(gT_all[:, g], ps[:, 6 + b], ACT.Copy).then_inc(c_gk, 1)

            sweep(act, [(1, high_g), (0, gates), (-1, keep_h), (-3, keep_g)], STEPS)
            if upto < 3:
                return

            act.wait_ge(c_x2, NG)

            def keep_HT(g, b, _):
                act.wait_ge(d_HT, g + 1)
                back(act, d_o, g - 1)
                act.activation(hT_s[:, b].rearrange("p j e -> p (j e)"), ps[:, 2 + b], ACT.Copy).then_inc(d_HTk, 1)

            sweep(act, [(1, ln_apply(D_PH, h_s, lambda g, b: back(act, d_HT, g - 1), True)), (0, keep_HT)])
            if upto < 4:
                return

            for k in range(2):
                rows = slice(k * LOW, (k + 1) * LOW)
                pick = ident[rows, rows].rearrange("p (j h) -> p h j", h=HEADS).unsqueeze(3)
                act.activation(qsel[rows].rearrange("p (h j m) -> p h j m", h=HEADS, j=GW),
                               pick.to_broadcast([LOW, HEADS, GW, P]), ACT.Copy).then_inc(e_qsel, 1)

            def exponent(g, b, h):
                u = g * HEADS + h
                q = h % 2
                act.wait_ge(u_Z, u + 1)
                back(act, u_P, u - 1)
                act.activation(E_u[:, q], Z_u[:, q], ACT.Exp).then_inc(u_E, 1)

            def keep_A(g, b, h):
                u = g * HEADS + h
                q = h % 2
                act.wait_ge(u_T, u + 1)
                back(act, u_AV, u - 1)
                act.activation(flat(A_u[:, q]), ps[:, 2 + q], ACT.Copy).then_inc(u_A, 1)

            def tanh(g, b, h):
                if h == HEADS - 1:
                    act.wait_ge(e_o, g + 1)
                    back(act, e_sg, g - 1)
                    act.activation(t_s[:, b], o_s[:, b], ACT.Tanh, scale=0.5).then_inc(e_th, 1)

            def free_he(g, b):
                back(act, e_hc, g - 1)
                back(act, e_T, g - 1)
                act.wait_ge(d_T, NG)

            def keep_V(g, b, c):
                act.wait_ge(e_V, g * HEADS + c + 1)
                back(act, u_AV, (g - 1) * HEADS)
                act.activation(V[:, b, c // 2, (c % 2) * 512:(c % 2) * 512 + 512], ps[:, 7 - c % 2],
                               ACT.Copy).then_inc(e_Vk, 1)

            apply_e = ln_apply(E_PH, he_s, free_he)

            def group(g, b):
                for h in range(HEADS):
                    if h == 0 and has(g + 1):
                        act.wait_ge(e_k, g + 2)
                        back(act, e_K, g)
                        act.activation(flat(kf_s[:, 1 - b])[0:LOW + HEADS], ps[0:LOW + HEADS, 7], ACT.Identity,
                                       bias=ck[0:LOW + HEADS]).then_inc(e_kb, 1)
                        act.wait_ge(e_q, g + 2)
                        back(act, e_Q, g)
                        act.activation(qf_s[0:2 * LOW, 1 - b, 0:P], ps[0:2 * LOW, 6, 0:P], ACT.Identity,
                                       bias=cq[0:2 * LOW]).then_inc(e_qb, 1)
                    units(g, b, h, [(1, exponent), (3, keep_A), (5, tanh)])
                    value_chunk(g, b, h, keep_V)
                    if h == 3 and has(g + 2):
                        apply_e(g + 2, b, 0)
                    if h == 4 and has(g + 2):
                        act.wait_ge(e_T, g + 3)
                        back(act, e_split, g + 1)
                        back(act, e_q, g + 1)
                        act.activation(flat(heT_s[:, b]), ps[:, 6], ACT.Copy).then_inc(e_hT, 1)

            all_groups(act, group)

        @block.tensor
        def _(pe):
            pe.wait_ge(w_in, 16 * len(WLOADS))
            pe.wait_ge(p_id, 1)
            for k, tile in enumerate(tiles):
                n = tile.shape[0]
                last = pe.transpose(ps[:, k // 4, (k % 4) * P:(k % 4) * P + n], tile, ident[0:n, 0:n])
                if k % 4 == 3 or k == NT - 1:
                    last.then_inc(p_T, 1)
            pe.wait_ge(p_bld, 1)
            pe.wait_ge(p_Tc, TB)

            def tT(k):
                return sT[:, k * P:(k + 1) * P]

            pe.matmul(ps[:, 5, 0:2], r_w0, r_a, start=True, stop=True)
            pe.matmul(ps[:, 5, 2:4], b0rep, r_a, start=True, stop=True)
            for h in range(HEADS):
                pe.matmul(ps[:, 5, 8 + 2 * h:10 + 2 * h], tT(T_FC + h), r_qk, start=True, stop=True)
            pe.matmul(ps[0:LOW + HEADS, 5, 32:33], fcbk[:, 0:LOW + HEADS], r_qk[:, 1:2], start=True, stop=True)
            pe.matmul(ps[0:2 * LOW, 5, 33:34], fcbq, r_qk[:, 0:1], start=True, stop=True)
            for h in range(HEADS):
                last = pe.matmul(ps[:, 5, 128:256], fcbrep[:, h], r_fp[:, h], start=(h == 0), stop=(h == HEADS - 1))
            last.then_inc(p_mm, 1)
            for l in range(STEPS):
                pe.matmul(ps[:, l, 0:3 * P], tT(T_GW + l), sT[:, T_WIH * P:(T_WIH + 3) * P], start=True, stop=True)
            for h in range(HEADS):
                last = pe.matmul(ps[:, 6 + h // 4, (h % 4) * P:(h % 4) * P + P], tT(T_FC + h), r_fp[:, h],
                                 start=True, stop=True)
            last.then_inc(p_mm, 1)
            pe.wait_ge(p_done, 1)
            pe.wait_ge(a_ycol, 1)

            def transposes(g, b, _):
                pe.wait_ge(ln_h, g + 1)
                pe.wait_ge(a_ld[b], (g - b) * 8 + 16)
                back(pe, a_adjT, g)
                for j in range(GW):
                    pe.transpose(ps[:, 0, j * P:(j + 1) * P], h_s[:, b, j], ident[:, :])
                for j in range(GW):
                    last = pe.transpose(ps[:, 1, j * P:(j + 1) * P], adj_s[:, b, j], ident[:, :])
                last.then_inc(a_T, 1)

            def project(g, b, _):
                pe.wait_ge(a_hT, g + 1)
                back(pe, a_Y, g)
                for j in range(GW):
                    o = (j % 2) * 256
                    last = pe.matmul(ps[:, 2 + j // 2, o:o + P + 2], hT_s[:, b, j], W0e[:, :], start=True, stop=True)
                last.then_inc(a_proj, 1)

            def aggregate(g, b, _):
                pe.wait_ge(a_Y, g + 1)
                pe.wait_ge(a_adjT, g + 1)
                back(pe, a_x1, g)
                for j in range(GW):
                    o = (j % 2) * 256
                    last = pe.matmul(ps[:, 4 + j // 2, o:o + P + 2], adjT_s[:, b, j], Y_s[b][:, j], start=True, stop=True)
                last.then_inc(a_agg, 1)

            sweep(pe, [(1, transposes), (0, project), (-1, aggregate)])
            if upto < 2:
                return

            def b_trans(g, b, _):
                pe.wait_ge(ln_h, NG * B_PH + g + 1)
                back(pe, b_hT, g - 1)
                for j in range(GW):
                    last = pe.transpose(ps[:, b, j * P:(j + 1) * P], w1[6][:, b, j], ident[:, :])
                last.then_inc(b_T, 1)

            def b_agg(g, b, _):
                pe.wait_ge(a_edges, NG)
                back(pe, b_gT, g - 1)
                for j in range(GW):
                    last = pe.matmul(ps[:, 6 + b, j * P:(j + 1) * P], w1[6][:, b, j], edges[:, g, j], start=True, stop=True)
                last.then_inc(b_g, 1)

            sweep(pe, [(0, b_trans), (0, b_agg)])

            def three(bank, w, col, src, b, start, stop, l):
                hi, lo = gru_w[:, 0, w, col * P:(col + 1) * P], gru_w[:, 1, w, col * P:(col + 1) * P]
                pe.matmul(ps[:, bank], hi, split[:, b, src], start=start, stop=False)
                pe.matmul(ps[:, bank], lo, split[:, b, src], start=False, stop=False)
                return pe.matmul(ps[:, bank], hi, split[:, b, src + 1], start=False, stop=stop)

            def gate_products(g, b, l):
                t = g + NG * l
                pe.wait_ge(c_hsp, t + 1)
                back(pe, c_sr, t)
                if l == 0:
                    pe.wait_ge(b_hT, NG)
                three(0, STEPS, 0, 0, b, True, False, l)
                pe.wait_ge(c_glo, t + 1)
                three(0, l, 0, 2, b, False, True, l).then_inc(c_r, 1)
                back(pe, c_t1, t)
                three(1, STEPS, 2, 0, b, True, True, l).then_inc(c_hn, 1)
                back(pe, c_t2, t)
                three(2, l, 2, 2, b, True, True, l).then_inc(c_in, 1)
                back(pe, c_sz, t)
                three(3, STEPS, 1, 0, b, True, False, l)
                three(3, l, 1, 2, b, False, True, l).then_inc(c_z, 1)

            def c_trans(g, b, l):
                t = g + NG * l
                pe.wait_ge(c_h, t + 1)
                if l < STEPS - 1:
                    back(pe, c_nat, t - 1)
                else:
                    pe.wait_ge(c_nat, NG * (STEPS - 1))
                    back(pe, c_x2, g - 1)
                for j in range(GW):
                    last = pe.transpose(ps[:, 4 + b, j * P:(j + 1) * P], w1[5][:, b, j], ident[:, :])
                last.then_inc(c_T, 1)

            def c_agg(g, b, l):
                if l == STEPS - 1:
                    return
                t = g + NG * l
                pe.wait_ge(c_nat, t + 1)
                if l == 0:
                    pe.wait_ge(b_gT, NG)
                back(pe, c_gk, t - 1)
                for j in range(GW):
                    last = pe.matmul(ps[:, 6 + b, j * P:(j + 1) * P], w1[6][:, b, j], edges[:, g, j], start=True, stop=True)
                last.then_inc(c_g, 1)

            sweep(pe, [(0, gate_products), (-1, c_trans), (-2, c_agg)], STEPS)
            if upto < 3:
                return

            pe.wait_ge(c_x2, NG)

            def d_trans(g, b, _):
                pe.wait_ge(d_ld[b], (g - b) * 8 + 16)
                back(pe, d_adjT, g - 1)
                for j in range(GW):
                    last = pe.transpose(ps[:, b, j * P:(j + 1) * P], adj_s[:, b, j], ident[:, :])
                last.then_inc(d_T, 1)

            def d_agg(g, b, _):
                pe.wait_ge(d_adjT, g + 1)
                pe.wait_ge(ln_h, NG * D_PH + g + 1)
                back(pe, d_HTk, g - 1)
                for j in range(GW):
                    last = pe.matmul(ps[:, 2 + b, j * P:(j + 1) * P], h_s[:, b, j], adjT_s[:, b, j], start=True, stop=True)
                last.then_inc(d_HT, 1)

            def d_project(g, b, _):
                pe.wait_ge(d_HTk, g + 1)
                back(pe, d_t, g - 1)
                for j in range(GW):
                    last = pe.matmul(ps[:, 4 + b, j * P:(j + 1) * P], hT_s[:, b, j], W2T[:, :], start=True, stop=True)
                last.then_inc(d_o, 1)

            sweep(pe, [(1, d_trans), (0, d_agg), (-1, d_project)])
            if upto < 4:
                return

            pe.wait_ge(d_x3, NG)

            def logits(g, b, h):
                u = g * HEADS + h
                q = h % 2
                pe.wait_ge(e_qsel, 2)
                pe.wait_ge(e_K, g + 1)
                pe.wait_ge(e_Q, g + 1)
                back(pe, u_X, u - 1)
                pe.matmul(ps[:, q], split[0:2 * LOW, b, 3, 0:P], qsel[:, h * ROWS:(h + 1) * ROWS], start=True, stop=False)
                pe.matmul(ps[:, q], selk[:, h], split[0:LOW + HEADS, b, 2], start=False, stop=True).then_inc(u_S, 1)

            def probs_T(g, b, h):
                u = g * HEADS + h
                q = h % 2
                pe.wait_ge(u_P, u + 1)
                back(pe, u_A, u - 1)
                for j in range(GW):
                    last = pe.transpose(ps[:, 2 + q, j * P:(j + 1) * P], P_u[:, q, j], ident[:, :])
                last.then_inc(u_T, 1)

            def attend(g, b, h):
                u = g * HEADS + h
                q = h % 2
                pe.wait_ge(u_A, u + 1)
                pe.wait_ge(e_Vk, (g + 1) * HEADS)
                if h == 0:
                    back(pe, e_o, g - 1)
                for j in range(GW):
                    last = pe.matmul(ps[:, 4 + b, j * P:(j + 1) * P], A_u[:, q, j], V[:, b, j, h * P:(h + 1) * P],
                                     start=(h == 0 and j == 0), stop=(h == HEADS - 1), skip_group_check=True)
                last.then_inc(u_AV, 1)

            def values(g, b, c):
                pe.wait_ge(e_split, g + 1)
                back(pe, e_Vk, g * HEADS + c - 1)
                j, bank, cols = c // 2, 7 - c % 2, slice((c % 2) * 512, (c % 2) * 512 + 512)
                hi, lo = (split[:, b, k, j * P:(j + 1) * P] for k in range(2))
                pe.matmul(ps[:, bank], hi, G[:, 0, cols], start=True, stop=False)
                pe.matmul(ps[:, bank], lo, G[:, 0, cols], start=False, stop=False)
                pe.matmul(ps[:, bank], hi, G[:, 1, cols], start=False, stop=True).then_inc(e_V, 1)

            def group(g, b):
                for h in range(HEADS):
                    units(g, b, h, [(0, logits), (3, probs_T), (4, attend)])
                    if h == 0 and has(g + 1):
                        pe.wait_ge(e_hT, g + 2)
                        back(pe, e_Vk, g * HEADS + 3)
                        pe.matmul(ps[0:LOW + HEADS, 7], Wk[:, :], flat(heT_s[:, 1 - b]), start=True, stop=True).then_inc(e_k, 1)
                        back(pe, e_Vk, g * HEADS + 4)
                        for j in range(GW):
                            last = pe.matmul(ps[0:2 * LOW, 6, 0:P], Wq[:, j], heT_s[:, 1 - b, j], start=(j == 0), stop=(j == GW - 1))
                        last.then_inc(e_q, 1)
                    if h == 0 and has(g + 1):
                        pe.wait_ge(e_kb, g + 2)
                    if h == 1 and has(g + 1):
                        pe.wait_ge(e_qb, g + 2)
                    if h == 5 and has(g + 2):
                        pe.wait_ge(e_hT, g + 3)
                    value_chunk(g, b, h, values)
                    if h == 4 and has(g + 2):
                        pe.wait_ge(ln_h, NG * E_PH + (g + 2) + 1)
                        back(pe, e_Vk, HEADS * (g + 1))
                        for j in range(GW):
                            last = pe.transpose(ps[:, 6, j * P:(j + 1) * P], he_s[:, b, j], ident[:, :])
                        last.then_inc(e_T, 1)

            all_groups(pe, group)


_INS = ["x", "adj", "nodemask", "L0_gnn_W_w", "L0_gnn_W_b", "L0_gnn_a_w", "L0_gnn_a_b", "L1_gnn_weight", "L1_gnn_w_ih",
        "L1_gnn_w_hh", "L1_gnn_b_ih", "L1_gnn_b_hh", "L2_gnn_W", "L2_gnn_b", "L3_gnn_fc_w", "L3_gnn_fc_b", "L3_gnn_q_w",
        "L3_gnn_q_b", "L3_gnn_k_w", "L3_gnn_k_b", "L3_gnn_fp_w", "L3_gnn_fp_b"]


def kernel(**inputs):
    import numpy as _np
    import concourse.bacc as _bacc
    from concourse import mybir as _mybir
    from concourse.bass_utils import run_bass_kernel_spmd as _run

    nc = _bacc.Bacc("TRN2", target_bir_lowering=False, num_devices=1)
    arrays, args = {}, []
    for name in _INS:
        a = _np.ascontiguousarray(inputs[name])
        arrays[f"in_{name}"] = a
        args.append(nc.dram_tensor(f"in_{name}", a.shape, _mybir.dt.from_np(a.dtype), kind="ExternalInput").ap())
    o = nc.dram_tensor("out_x", (GRAPHS, P, P), F32, kind="ExternalOutput").ap()
    build(nc, *args, o)
    r = _run(nc, [arrays], core_ids=[0])
    return r.results[0]["out_x"]
```

```python
from contextlib import ExitStack

import concourse.bass as bass
from concourse import mybir

F32 = mybir.dt.float32
F32R = mybir.dt.float32r
ALU = mybir.AluOpType
ACT = mybir.ActivationFunctionType
AX = mybir.AxisListType

P = 128
GRAPHS = 64
GW = 4
NG = GRAPHS // GW
HEADS = 8
STEPS = 5
EPS = 1e-5
NEG = -1e9
SLOPE = 0.01
ROWS = GW * P
LOW = 32
A_PH, B_PH, D_PH, E_PH = range(4)


def by_pairs(stage):
    return lambda g, place, block: stage(g, place % 2, block)


def back(eng, sem, value):
    if isinstance(value, int) and value <= 0:
        return
    eng.wait_ge(sem, value)


def alone(eng, met):
    eng.sem_inc(met, 1)


def sweep(eng, stages, blocks=1, n=NG, ring=2):
    lead = max(0, max(o for o, _ in stages))
    lag = max(0, -min(o for o, _ in stages))
    first = -(-(2 + lag) // ring) * ring
    last = (n - lead) // ring * ring

    def written_out(i):
        for o, stage in stages:
            t = i + o
            if 0 <= t < n * blocks:
                stage(t % n, t % ring, t // n)

    for i in range(-lead, 0):
        written_out(i)
    for block in range(blocks):
        for g in range(0, first):
            written_out(block * n + g)
        with eng.Fori(first // ring, last // ring) as turn:
            for place in range(ring):
                for o, stage in stages:
                    stage(turn * ring + (place + o), (place + o) % ring, block)
        for g in range(last, n):
            written_out(block * n + g)
    for i in range(n * blocks, n * blocks + lag):
        written_out(i)


def build(nc, x_in, adj_in, mask_in, w0_in, b0_in, a_in, ab_in, gw_in, wih_in, whh_in, bih_in, bhh_in,
          w2_in, b2_in, fc_in, fcb_in, qw_in, qb_in, kw_in, kb_in, fp_in, fpb_in, out, upto=4):
    with ExitStack() as ctx:
        def sb(name, shape, dt=F32):
            return ctx.enter_context(nc.sbuf_tensor(name, shape, dt))

        def sem(name):
            return ctx.enter_context(nc.semaphore(name))

        x_all = sb("x_all", [P, NG, GW, P])
        ident = sb("ident", [P, P])
        half = sb("half", [P, GW])
        edges = sb("edges", [P, NG, GW, P])
        hT_all = sb("hT_all", [P, NG, ROWS])
        gT_all = sb("gT_all", [P, NG, ROWS])
        W0e = sb("W0e", [P, P + 2])
        c0 = sb("c0", [P, 2])
        b0row = sb("b0row", [P, P])
        ab = sb("ab", [P, 1])
        gru_w = sb("gru_w", [P, 2, STEPS + 1, 3 * P], F32R)
        gate_b = sb("gate_b", [P, 4])
        maskT = sb("maskT", [P, GRAPHS])
        W2T = sb("W2T", [P, P])
        b2row = sb("b2row", [P, P])
        deg = sb("deg", [P, NG, GW])
        G = sb("G", [P, 2, HEADS * P], F32R)
        Wk = sb("Wk", [P, LOW + HEADS])
        Wq = sb("Wq", [P, GW, 2 * LOW])
        ck = sb("ck", [P, 1])
        cq = sb("cq", [P, 1])
        ce = sb("ce", [P, P])
        selk = sb("selk", [LOW + HEADS, HEADS, P], F32R)
        bn = sb("bn", [P, 2, GW, 6])
        mv = sb("mv", [P, 2, GW, 2])
        ve = sb("ve", [P, 2, GW])
        rstd = sb("rstd", [P, 2, GW])
        nmr = sb("nmr", [P, 2, GW])
        w1 = [sb(f"work{i}", [P, 2, GW, P]) for i in range(7)]
        split = sb("split", [P, 2, 4, ROWS], F32R)
        small = sb("small", [P, 2, 8, GW])
        ps = ctx.enter_context(nc.psum_tensor("ps", [P, 8, 512], F32))

        st = hT_all[:, :, :].rearrange("p a b -> p (a b)")
        sT = gT_all[:, :, :].rearrange("p a b -> p (a b)")
        r_w0, r_w2, r_mask = st[:, 0:128], st[:, 128:256], st[0:GRAPHS, 256:384]
        r_gw = st[:, 384:1024].rearrange("p (l e) -> p l e", e=P)
        r_wih = st[:, 1024:1408].rearrange("p (l e) -> p l e", e=P)
        r_whh = st[:, 1408:1792].rearrange("p (l e) -> p l e", e=P)
        r_fc = st[:, 1792:2816].rearrange("p (l e) -> p l e", e=P)
        r_fp = st[:, 6272:7296].rearrange("p (l e) -> p l e", e=P)
        r_vec = st[0:19, 3712:3840]
        vec0 = (9 + STEPS + HEADS) * P
        r_a, r_b0 = sT[:, vec0:vec0 + 2], sT[:, vec0 + 2:vec0 + 3]
        r_bih, r_bhh = sT[:, vec0 + 3:vec0 + 6], sT[:, vec0 + 6:vec0 + 9]
        r_fcb, r_qk = sT[:, vec0 + 9:vec0 + 17], sT[:, vec0 + 17:vec0 + 19]
        adj4 = sT[:, 8 * ROWS:12 * ROWS].rearrange("p (b j e) -> p b j e", b=4, j=GW)
        ef = sT[:, (NG - 1) * ROWS:(NG - 1) * ROWS + NG * GW].rearrange("p (g j) -> p g j", g=NG)
        r_qb, r_kb = st[:, 3859:3860], st[:, 3860:3861]
        b0rep = st[:, 3968:4096]
        fcbk = st[:, 4096:4096 + 64]
        fcbq = st[:, 4160:4160 + 64]
        fcbrep = st[:, 4224:4224 + 1024].rearrange("p (h e) -> p h e", e=P)
        tiles = [r_w0, r_w2, r_mask, r_whh[:, 0], r_whh[:, 1], r_whh[:, 2], r_wih[:, 0], r_wih[:, 1], r_wih[:, 2]]
        tiles += [r_gw[:, l] for l in range(STEPS)] + [r_fc[:, h] for h in range(HEADS)] + [r_vec]
        T_W0, T_W2, T_MASK, T_WHH, T_WIH, T_GW, T_FC = 0, 1, 2, 3, 6, 9, 9 + STEPS
        NT = len(tiles)
        TB = -(-NT // 4)
        assert TB <= 6

        w_in, p_id0, p_id = sem("weights_in"), sem("prep_ident_zero"), sem("prep_ident")
        p_T, p_Tc, p_bld = sem("prep_transposed"), sem("prep_transposes_kept"), sem("prep_built")
        p_mm, p_hi, p_done = sem("prep_products"), sem("prep_high"), sem("prep_done")
        p_zero = sem("prep_zeroed")
        p_ahi = sem("prep_act_high")
        dve_met, pool_met = sem("vector_waits_met"), sem("gpsimd_waits_met")
        ln_bn, ln_mv, ln_ve = sem("ln_bn"), sem("ln_mv"), sem("ln_ve")
        ln_rstd, ln_nmr, ln_h = sem("ln_rstd"), sem("ln_nmr"), sem("ln_h")
        x_ld = [sem(f"x_landed{i}") for i in range(2)]
        a_ld = [sem(f"adj_landed{i}") for i in range(4)]
        a_T, a_Ta, a_adjT, a_hT = sem("a_h_transposed"), sem("a_adj_transposed"), sem("a_adjT_kept"), sem("a_hT_kept")
        a_proj, a_exp, a_Y, a_agg = sem("a_projected"), sem("a_exps"), sem("a_Y"), sem("a_aggregated")
        a_edges, a_xb, a_s1, a_s2, a_s3 = sem("a_edges"), sem("a_xb"), sem("a_den"), sem("a_rden"), sem("a_scale")
        a_x1 = sem("a_x1")
        a_ycol = sem("a_ycol")
        b_T, b_hT, b_g, b_gT = sem("b_transposed"), sem("b_hT_kept"), sem("b_aggregated"), sem("b_gT_kept")
        c_hhi, c_hsp, c_ghi, c_glo = sem("c_h_high"), sem("c_h_split"), sem("c_g_high"), sem("c_g_low")
        c_r, c_hn, c_in, c_z = sem("c_r_ready"), sem("c_hn_ready"), sem("c_in_ready"), sem("c_z_ready")
        c_sr, c_sz, c_t1, c_t2, c_n = sem("c_r"), sem("c_z"), sem("c_t1"), sem("c_t2"), sem("c_n")
        c_d, c_zd, c_h = sem("c_h_minus_n"), sem("c_z_times"), sem("c_h_new")
        c_hk, c_T, c_nat, c_g, c_gk = sem("c_h_kept"), sem("c_transposed"), sem("c_nat"), sem("c_aggregated"), sem("c_g_kept")
        c_x2 = sem("c_x2")
        d_ld = [sem(f"d_adj_landed{i}") for i in range(4)]
        d_pow, d_dscale, d_T, d_adjT = sem("d_pow"), sem("d_scale"), sem("d_transposed"), sem("d_adjT")
        d_HT, d_HTk, d_o, d_t, d_t1, d_x3 = (sem("d_HT"), sem("d_HT_kept"), sem("d_out"), sem("d_scaled"),
                                             sem("d_biased"), sem("d_x3"))
        e_ld = [sem(f"e_adj_landed{i}") for i in range(2)]
        e_qsel = sem("e_qsel")
        e_T, e_hT, e_hhi, e_split = sem("e_transposed"), sem("e_hT_kept"), sem("e_h_high"), sem("e_h_split")
        e_k, e_kb, e_khi, e_K = sem("e_k"), sem("e_k_biased"), sem("e_k_high"), sem("e_K_rows")
        e_q, e_qb, e_qhi, e_Q = sem("e_q"), sem("e_q_biased"), sem("e_q_high"), sem("e_Q_rows")
        e_V, e_Vk, e_M, e_hc = sem("e_V"), sem("e_V_kept"), sem("e_M"), sem("e_hc")
        e_o, e_th, e_sg, e_x4 = sem("e_o"), sem("e_tanh"), sem("e_sigmoid"), sem("e_x4")
        u_neg = sem("u_negated")
        u_S, u_X, u_mx, u_Y, u_Z, u_E = sem("u_S"), sem("u_X"), sem("u_max"), sem("u_leaky"), sem("u_shifted"), sem("u_exp")
        u_s, u_r, u_P, u_T, u_A, u_AV = sem("u_sum"), sem("u_rsum"), sem("u_probs"), sem("u_T"), sem("u_A_kept"), sem("u_AV")
        o_st = sem("out_stored")

        block = ctx.enter_context(nc.Block())

        def bcast(ap, n=GW):
            return ap.unsqueeze(1).to_broadcast([ap.shape[0], n, ap.shape[1]])

        def along(ap, n=P):
            return ap.unsqueeze(2).to_broadcast([ap.shape[0], ap.shape[1], n])

        WLOADS = [
            (r_w0, w0_in), (r_w2, w2_in), (r_mask, mask_in),
            (r_whh, whh_in.rearrange("(k r) d -> r k d", r=P)), (r_wih, wih_in.rearrange("(k r) d -> r k d", r=P)),
            (r_gw, gw_in.rearrange("l d e -> d l e")), (r_fc, fc_in.rearrange("d (h e) -> d h e", e=P)),
            (r_fp, fp_in.rearrange("(h c) e -> c h e", c=P)),
            (r_vec[0:2], a_in.rearrange("(t e) -> t e", e=P)), (r_vec[2:3], b0_in.rearrange("(t e) -> t e", e=P)),
            (r_vec[3:6], bih_in.rearrange("(t e) -> t e", e=P)), (r_vec[6:9], bhh_in.rearrange("(t e) -> t e", e=P)),
            (r_vec[9:17], fcb_in.rearrange("(t e) -> t e", e=P)), (r_vec[17:18], qw_in.rearrange("e t -> t e")),
            (r_vec[18:19], kw_in.rearrange("e t -> t e")),
            (r_qb, qb_in.partition_broadcast(P)), (r_kb, kb_in.partition_broadcast(P)),
            (ab[:, :], ab_in.partition_broadcast(P)), (b0row[:, :], b0_in.partition_broadcast(P)),
            (b2row[:, :], b2_in.partition_broadcast(P)), (ce[:, :], fpb_in.partition_broadcast(P)),
        ]

        x_dram = x_in.rearrange("(g j) n d -> n g j d", j=GW)
        adj_dram = adj_in.rearrange("(g j) n m -> n g j m", j=GW)
        out_dram = out.rearrange("(g j) n d -> n g j d", j=GW)
        adj_s, h_s, hT_s, adjT_s, xb_s = w1[0], w1[1], w1[2], w1[3], w1[4]
        Y_s = [w1[5][:, :, :, :].rearrange("p b j e -> p (b j e)")[:, 0:GW * (P + 2)].rearrange("p (j e) -> p j e", e=P + 2),
               w1[6][:, :, :, :].rearrange("p b j e -> p (b j e)")[:, 0:GW * (P + 2)].rearrange("p (j e) -> p j e", e=P + 2)]

        qsel = gru_w[:, :, :, :].rearrange("p a w c -> p (a w c)")[0:2 * LOW, 0:HEADS * ROWS]
        V = st.rearrange("p (b j c) -> p b j c", b=2, j=GW)
        unit = edges[:, :, :, :].rearrange("p (k b) j e -> p k b j e", b=2)
        X_u, Z_u, E_u = (unit[:, k] for k in range(3))
        P_u, A_u = (unit[:, k:k + 2].rearrange("p k b j e -> p (k b) j e") for k in (3, 5))
        he_s, heT_s, M_s, kf_s = w1[1], w1[2], w1[3], w1[4]
        spare = gT_all[:, :, :].rearrange("p (k b) r -> p k b r", b=2)
        hc_s, o_s, t_s, g_s, qf_s = (spare[:, k] for k in range(5))
        sm = small

        def flat(ap):
            return ap.rearrange("p j e -> p (j e)")

        def units(g, b, h, stages):
            for lag, stage in stages:
                if lag > h:
                    if not (isinstance(g, int) and g <= 0):
                        stage(g - 1, 1 - b, h - lag + HEADS)
                elif not (isinstance(g, int) and not 0 <= g < NG):
                    stage(g, b, h - lag)

        def has(g):
            return not isinstance(g, int) or 0 <= g < NG

        def value_chunk(g, b, h, stage):
            if h >= HEADS // 2:
                g, b, c = g + 1, 1 - b, h - HEADS // 2
            else:
                c = h + HEADS // 2
            if has(g):
                stage(g, b, c)

        def all_groups(eng, group):
            for g in range(-2, 4):
                group(g, g % 2)
            with eng.Fori(2, NG // 2 - 1) as pair:
                for b in range(2):
                    group(pair * 2 + b, b)
            for g in (NG - 2, NG - 1, NG):
                group(g, g % 2)

        @block.sync
        def _(sp):
            for dst, src in WLOADS[:11]:
                sp.dma_start(dst, src).then_inc(w_in, 16)

            def load_x(g, b, _):
                back(sp, x_ld[b], (g - b) * 8)
                sp.dma_start(x_all[:, g], x_dram[:, g]).then_inc(x_ld[b], 16)

            def load_adj(g, q, _):
                back(sp, a_edges, g - 3)
                back(sp, a_Ta, g - 3)
                sp.dma_start(adj4[:, q], adj_dram[:, g]).then_inc(a_ld[q], 16)

            sweep(sp, [(4, by_pairs(load_x)), (2, load_adj)], ring=4)

            if upto >= 3:
                sp.wait_ge(c_glo, NG * (STEPS - 1) + 12)

                def load_adj2(g, q, _):
                    back(sp, d_T, g - 3)
                    sp.dma_start(adj4[:, q], adj_dram[:, g]).then_inc(d_ld[q], 16)

                sweep(sp, [(0, load_adj2)], ring=4)

            if upto >= 4:
                sp.wait_ge(d_T, NG)

                def load_adj3(g, b, _):
                    back(sp, e_M, g - 1)
                    sp.dma_start(adj_s[:, b], adj_dram[:, g]).then_inc(e_ld[b], 16)
                    if isinstance(g, int) and g < 2:
                        return
                    sp.wait_ge(e_x4, g - 1)
                    sp.dma_start(out_dram[:, g - 2], x_all[:, g - 2]).then_inc(o_st, 16)

                sweep(sp, [(0, load_adj3)])
                for g in (NG - 2, NG - 1):
                    sp.wait_ge(e_x4, g + 1)
                    sp.dma_start(out_dram[:, g], x_all[:, g]).then_inc(o_st, 16)
                sp.wait_ge(o_st, 16 * NG)
                return

            final = {1: a_x1, 2: c_x2, 3: d_x3, 4: e_x4}[upto]

            def store(g, b, _):
                sp.wait_ge(final, g + 1)
                sp.dma_start(out_dram[:, g], x_all[:, g]).then_inc(o_st, 16)

            sweep(sp, [(0, store)])
            sp.wait_ge(o_st, 16 * NG)

        @block.gpsimd
        def _(pool):
            pool.memset(ident[:, :], 0.0).then_inc(p_id0, 1)
            pool.memset(half[:, :], -0.5)
            pool.memset(fcbk, 0.0)
            pool.memset(Wk[:, :], 0.0)
            pool.memset(Wq[:, :, :], 0.0).then_inc(p_id0, 1)
            pool.wait_ge(p_id0, 2)
            pool.affine_select(out=ident[:, :], in_=ident[:, :], compare_op=ALU.not_equal, fill=1.0, base=0,
                               pattern=[[-1, P]], channel_multiplier=1).then_inc(p_id, 1)

            def ln_pow(ph):
                def stage(g, b, _):
                    t = g + NG * ph
                    pool.wait_ge(ln_ve, t + 1)
                    back(pool, ln_h, t - 1)
                    pool.tensor_tensor(rstd[:, b], ve[:, b], half[:, :], ALU.pow).then_inc(ln_rstd, 1)
                return stage

            def x_plus_b(g, b, _):
                pool.wait_ge(w_in, 16 * len(WLOADS))
                pool.wait_ge(x_ld[b], (g - b) * 8 + 16)
                back(pool, a_x1, g - 1)
                pool.tensor_tensor(xb_s[:, b], x_all[:, g], bcast(b0row[:, :]), ALU.add).then_inc(a_xb, 1)

            def deg_pow(g, b, _):
                pool.wait_ge(a_s3, g * 2 + 1)
                pool.tensor_tensor(deg[:, g], deg[:, g], half[:, :], ALU.pow).then_inc(d_pow, 1)

            sweep(pool, [(-1, x_plus_b), (4, ln_pow(A_PH)), (-3, deg_pow)])
            if upto < 2:
                return
            sweep(pool, [(0, ln_pow(B_PH))])

            def h_minus_n(g, b, l):
                t = g + NG * l
                pool.wait_ge(c_n, t + 1)
                back(pool, c_h, t - 1)
                pool.tensor_tensor(w1[4][:, b].rearrange("p j e -> p (j e)"), hT_all[:, g],
                                   w1[3][:, b].rearrange("p j e -> p (j e)"), ALU.subtract).then_inc(c_d, 1)
                pool.wait_ge(c_d, t + 1)
                pool.wait_ge(c_sz, t + 1)
                pool.tensor_tensor(w1[4][:, b], w1[4][:, b], w1[1][:, b], ALU.mult).then_inc(c_zd, 1)

            sweep(pool, [(0, h_minus_n)], STEPS)
            if upto < 3:
                return

            def add_b2(g, b, _):
                pool.wait_ge(d_t, g + 1)
                t = hT_all[:, g].rearrange("p (j e) -> p j e", e=P)
                pool.tensor_tensor(t, t, bcast(b2row[:, :]), ALU.add).then_inc(d_t1, 1)

            sweep(pool, [(-4, add_b2), (1, ln_pow(D_PH))])
            if upto < 4:
                return

            def shift(g, b, h):
                if h % 2:
                    return
                u = g * HEADS + h
                q = h % 2
                pool.wait_ge(u_Y, u + 1)
                back(pool, u_E, u - 1)
                pool.tensor_tensor(Z_u[:, q], X_u[:, q], along(sm[:, q, 1]), ALU.subtract).then_inc(u_Z, 1)

            def normalize(g, b, h):
                u = g * HEADS + h
                q = h % 2
                pool.wait_ge(u_r, u + 1)
                back(pool, u_T, u - 3)
                pool.tensor_tensor(P_u[:, h % 4], E_u[:, q], along(sm[:, q, 3]), ALU.mult).then_inc(u_P, 1)

            def sigmoid(g, b, h):
                if h == HEADS - 1:
                    pool.wait_ge(e_th, g + 1)
                    alone(pool, pool_met)
                    pool.tensor_scalar(g_s[:, b], t_s[:, b], 0.5, 0.5, ALU.mult, ALU.add).then_inc(e_sg, 1)

            def add_x(g, b, h):
                if h == HEADS - 1:
                    pool.wait_ge(e_sg, g + 1)
                    pool.tensor_tensor(x_all[:, g], g_s[:, b].rearrange("p (j e) -> p j e", e=P), x_all[:, g],
                                       ALU.add).then_inc(e_x4, 1)

            ln_pow_e = ln_pow(E_PH)

            def group(g, b):
                for h in range(HEADS):
                    units(g, b, h, [(2, normalize), (0, shift), (7, sigmoid), (8, add_x)])
                    if h == 2 and has(g + 2):
                        ln_pow_e(g + 2, b, 0)
                    if h == 4 and has(g + 1):
                        pool.wait_ge(e_ld[1 - b], (g + 1 - (1 - b)) * 8 + 16)
                        back(pool, u_X, g * HEADS)
                        alone(pool, pool_met)
                        pool.tensor_scalar(M_s[:, 1 - b], adj_s[:, 1 - b], -1.0, -NEG, ALU.add,
                                           ALU.mult).then_inc(e_M, 1)
                    if h == 7 and has(g + 1):
                        pool.wait_ge(ln_h, NG * E_PH + (g + 1) + 1)
                        back(pool, e_o, g)
                        pool.tensor_tensor(hc_s[:, 1 - b].rearrange("p (j e) -> p j e", e=P), he_s[:, 1 - b],
                                           bcast(ce[:, :]), ALU.add).then_inc(e_hc, 1)

            all_groups(pool, group)

        @block.vector
        def _(dve):
            def ln_stats(ph, ready):
                def stage(g, b, _):
                    t = g + NG * ph
                    ready(g, b)
                    for j in range(GW):
                        last = dve.bn_stats(bn[:, b, j], x_all[:, g, j])
                    last.then_inc(ln_bn, 1)
                    dve.wait_ge(ln_bn, t + 1)
                    back(dve, ln_nmr, t - 1)
                    alone(dve, dve_met)
                    for j in range(GW):
                        last = dve.bn_aggr(mv[:, b, j], bn[:, b, j])
                    last.then_inc(ln_mv, 1)
                    dve.wait_ge(ln_mv, t + 1)
                    back(dve, ln_rstd, t - 1)
                    dve.tensor_scalar(ve[:, b], mv[:, b, :, 1], EPS, None, ALU.add).then_inc(ln_ve, 1)
                return stage

            def ln_shift(ph, gcn=False):
                def stage(g, b, _):
                    t = g + NG * ph
                    dve.wait_ge(ln_rstd, t + 1)
                    back(dve, ln_h, t - 1)
                    if gcn:
                        dve.tensor_tensor(small[:, b, 7], rstd[:, b], deg[:, g], ALU.mult).then_inc(d_dscale, 1)
                        dve.wait_ge(d_dscale, g + 1)
                        dve.scalar_tensor_tensor(nmr[:, b], mv[:, b, :, 0], -1.0, small[:, b, 7], ALU.mult,
                                                 ALU.mult).then_inc(ln_nmr, 1)
                    else:
                        dve.scalar_tensor_tensor(nmr[:, b], mv[:, b, :, 0], -1.0, rstd[:, b], ALU.mult,
                                                 ALU.mult).then_inc(ln_nmr, 1)
                return stage

            dve.wait_ge(w_in, 16 * len(WLOADS))
            dve.wait_ge(p_id0, 2)
            dve.wait_ge(p_id, 1)
            dve.tensor_copy(selk[0:LOW], along(ident[0:LOW, 0:HEADS]))
            dve.tensor_copy(selk[LOW:LOW + HEADS], along(ident[LOW:LOW + HEADS, LOW:LOW + HEADS]))
            for k in range(TB):
                n = min(4, NT - 4 * k) * P
                dve.wait_ge(p_T, k + 1)
                if k == 0:
                    dve.tensor_copy(sT[:, 0:256], ps[:, 0, 0:256])
                    dve.tensor_copy(maskT[:, :], ps[:, 0, 256:256 + GRAPHS])
                    dve.tensor_copy(sT[:, 384:512], ps[:, 0, 384:512]).then_inc(p_Tc, 1)
                elif k == TB - 1:
                    dve.tensor_copy(sT[:, 512 * k:vec0], ps[:, k, 0:vec0 - 512 * k])
                    dve.tensor_copy(sT[:, vec0:vec0 + 19], ps[:, k, vec0 - 512 * k:vec0 - 512 * k + 19]).then_inc(p_Tc, 1)
                else:
                    dve.tensor_copy(sT[:, 512 * k:512 * k + n], ps[:, k, 0:n]).then_inc(p_Tc, 1)
            dve.wait_ge(p_Tc, TB)
            dve.tensor_copy(b0rep, r_b0.to_broadcast([P, P]))
            dve.tensor_copy(fcbrep, along(r_fcb))
            dve.tensor_copy(fcbk[:, 0:HEADS], r_fcb)
            dve.tensor_copy(fcbk[:, LOW:LOW + HEADS], r_fcb)
            dve.tensor_copy(fcbq.rearrange("p (k h) -> p k h", h=HEADS), bcast(r_fcb, 8))
            dve.tensor_copy(gate_b[:, 2:3], r_bih[:, 2:3])
            dve.tensor_copy(gate_b[:, 3:4], r_bhh[:, 2:3])
            dve.tensor_tensor(gate_b[:, 0:2], r_bih[:, 0:2], r_bhh[:, 0:2], ALU.add).then_inc(p_bld, 1)
            dve.tensor_copy(W0e[:, 0:P], sT[:, 0:P])
            dve.tensor_copy(W2T[:, :], sT[:, P:2 * P])
            whhT = sT[:, T_WHH * P:(T_WHH + 3) * P]
            dve.tensor_copy(gru_w[:, 0, STEPS], whhT).then_inc(p_hi, 1)
            dve.wait_ge(p_hi, 1)
            dve.tensor_tensor(gru_w[:, 1, STEPS], whhT, gru_w[:, 0, STEPS].bitcast(F32), ALU.subtract)
            dve.wait_ge(p_mm, 1)
            dve.tensor_copy(W0e[:, P:P + 2], ps[:, 5, 0:2])
            dve.tensor_copy(c0[:, :], ps[:, 5, 2:4]).then_inc(p_hi, 1)
            dve.wait_ge(p_hi, 2)
            dve.tensor_tensor(c0[:, 0:1], c0[:, 0:1], ab[:, :], ALU.add)
            wqk = ps[:, 5, 8:8 + 2 * HEADS].rearrange("p (h t) -> p t h", t=2)
            dve.tensor_copy(Wk[:, 0:HEADS], wqk[:, 1])
            dve.tensor_copy(Wk[:, LOW:LOW + HEADS], wqk[:, 1])
            for j in range(GW):
                for k in range(2):
                    o = k * LOW + j * HEADS
                    dve.tensor_copy(Wq[:, j, o:o + HEADS], wqk[:, 0])
            dve.tensor_tensor(ck[0:LOW + HEADS], ps[0:LOW + HEADS, 5, 32:33], r_kb[0:LOW + HEADS], ALU.add)
            dve.tensor_tensor(cq[0:2 * LOW], ps[0:2 * LOW, 5, 33:34], r_qb[0:2 * LOW], ALU.add)
            dve.tensor_tensor(ce[:, :], ps[:, 5, 128:256], ce[:, :], ALU.add)
            for l in range(STEPS):
                dve.wait_ge(p_ahi, l + 1)
                dve.tensor_tensor(gru_w[:, 1, l], ps[:, l, 0:3 * P], gru_w[:, 0, l].bitcast(F32), ALU.subtract)
            for k in range(2):
                dve.wait_ge(p_ahi, STEPS + k + 1)
                s = slice(512 * k, 512 * k + 512)
                last = dve.tensor_tensor(G[:, 1, s], ps[:, 6 + k], G[:, 0, s].bitcast(F32), ALU.subtract)
            last.then_inc(p_done, 1)
            dve.wait_ge(p_done, 1)

            for b in range(2):
                last = dve.memset(Y_s[b][:, :, P + 1:P + 2], 1.0)
            last.then_inc(a_ycol, 1)

            def take_edges(g, q, _):
                dve.wait_ge(a_ld[q], (g - q) * 4 + 16)
                dve.tensor_scalar(edges[:, g], adj4[:, q], 0.0, None, ALU.not_equal).then_inc(a_edges, 1)

            def finish(g, b, _):
                dve.wait_ge(a_agg, g + 1)
                agg = ps[:, 4:6, :].rearrange("p k (j e) -> p k j e", e=256)
                den = small[:, b, 2].rearrange("p (k j) -> p k j", j=2)
                dve.tensor_copy(den, agg[:, :, :, P])
                dve.tensor_scalar(deg[:, g].rearrange("p (k j) -> p k j", j=2), agg[:, :, :, P + 1], 1.0, None,
                                  ALU.add).then_inc(a_s3, 1)
                dve.wait_ge(a_s3, 2 * g + 1)
                dve.tensor_tensor(small[:, b, 2], small[:, b, 2], ef[:, g], ALU.mult).then_inc(a_s1, 1)
                dve.wait_ge(a_s1, g + 1)
                dve.reciprocal(small[:, b, 3], small[:, b, 2]).then_inc(a_s2, 1)
                dve.wait_ge(a_s2, g + 1)
                dve.tensor_tensor(small[:, b, 4], small[:, b, 3], ef[:, g], ALU.mult).then_inc(a_s3, 1)
                dve.wait_ge(a_s3, 2 * g + 2)
                dve.wait_ge(a_xb, g + 1)
                for j in range(GW):
                    last = dve.scalar_tensor_tensor(x_all[:, g, j], ps[:, 4 + j // 2, (j % 2) * 256:(j % 2) * 256 + P],
                                                    small[:, b, 4, j:j + 1], xb_s[:, b, j], ALU.mult, ALU.add)
                last.then_inc(a_x1, 1)

            x_landed = lambda g, b: dve.wait_ge(x_ld[b], (g - b) * 8 + 16)
            sweep(dve, [(-2, by_pairs(finish)), (3, by_pairs(ln_shift(A_PH))), (0, take_edges),
                        (4, by_pairs(ln_stats(A_PH, x_landed)))], ring=4)
            if upto < 2:
                return

            def keep_gT(g, b, _):
                dve.wait_ge(b_g, g + 1)
                dve.tensor_copy(gT_all[:, g], ps[:, 6 + b]).then_inc(b_gT, 1)

            sweep(dve, [(2, ln_shift(B_PH)), (0, keep_gT), (3, ln_stats(B_PH, lambda g, b: dve.wait_ge(a_x1, g + 1)))])

            def split_hg(g, b, l):
                t = g + NG * l
                if l == 0:
                    dve.wait_ge(b_hT, g + 1)
                    dve.wait_ge(b_gT, g + 1)
                else:
                    dve.wait_ge(c_hk, t - NG + 1)
                    dve.wait_ge(c_gk, t - NG + 1)
                back(dve, c_z, t - 1)
                dve.tensor_copy(split[:, b, 0], hT_all[:, g]).then_inc(c_hhi, 1)
                dve.wait_ge(c_hhi, t + 1)
                dve.tensor_tensor(split[:, b, 1], hT_all[:, g], split[:, b, 0].bitcast(F32),
                                  ALU.subtract).then_inc(c_hsp, 1)
                dve.wait_ge(c_ghi, t + 1)
                dve.tensor_tensor(split[:, b, 3], gT_all[:, g], split[:, b, 2].bitcast(F32),
                                  ALU.subtract).then_inc(c_glo, 1)

            def new_state(g, b, l):
                t = g + NG * l
                dve.wait_ge(c_zd, t + 1)
                back(dve, c_T, t - 1)
                back(dve, c_hk, t - 1)
                dve.tensor_tensor(w1[5][:, b], w1[3][:, b], w1[4][:, b], ALU.add).then_inc(c_h, 1)
                if l == STEPS - 1:
                    pass

            def candidate(g, b, l):
                t = g + NG * l
                dve.wait_ge(c_sr, t + 1)
                dve.wait_ge(c_hn, t + 1)
                back(dve, c_n, t - 1)
                tt = w1[2][:, b].rearrange("p j e -> p (j e)")
                dve.scalar_tensor_tensor(tt, ps[:, 1], gate_b[:, 3:4], w1[0][:, b].rearrange("p j e -> p (j e)"),
                                         ALU.add, ALU.mult).then_inc(c_t1, 1)
                dve.wait_ge(c_t1, t + 1)
                dve.wait_ge(c_in, t + 1)
                dve.tensor_tensor(tt, ps[:, 2], tt, ALU.add).then_inc(c_t2, 1)

            def to_x(g, b, l):
                if l < STEPS - 1:
                    return
                t = g + NG * l
                dve.wait_ge(c_T, t + 1)
                for j in range(GW):
                    o = g * GW + j
                    m = maskT[:, bass.ds(o, 1)]
                    last = dve.scalar_tensor_tensor(x_all[:, g, j], ps[:, 4 + b, j * P:(j + 1) * P], m,
                                                    x_all[:, g, j], ALU.mult, ALU.add)
                last.then_inc(c_x2, 1)

            sweep(dve, [(1, split_hg), (-1, new_state), (0, candidate), (-2, to_x)], STEPS)
            if upto < 3:
                return

            dve.wait_ge(d_pow, NG)

            def add_self(g, b, _):
                dve.wait_ge(d_T, g + 1)
                back(dve, d_HT, g - 1)
                dve.tensor_tensor(adjT_s[:, b], ps[:, b].rearrange("p (j e) -> p j e", e=P), bcast(ident[:, :]),
                                  ALU.add).then_inc(d_adjT, 1)

            def relu_add(g, b, _):
                dve.wait_ge(d_t1, g + 1)
                dve.scalar_tensor_tensor(x_all[:, g], hT_all[:, g].rearrange("p (j e) -> p j e", e=P), 0.0, x_all[:, g],
                                         ALU.max, ALU.add).then_inc(d_x3, 1)

            sweep(dve, [(0, add_self), (0, ln_shift(D_PH, True)), (-5, relu_add),
                        (1, ln_stats(D_PH, lambda g, b: dve.wait_ge(c_x2, g + 1)))])
            if upto < 4:
                return

            def mask_max(g, b, h):
                u = g * HEADS + h
                q = h % 2
                dve.wait_ge(u_S, u + 1)
                dve.wait_ge(e_M, g + 1)
                alone(dve, dve_met)
                for j in range(GW):
                    last = dve.tensor_tensor_reduce(X_u[:, q, j], ps[:, q, j * P:(j + 1) * P], M_s[:, b, j], 1.0, -3.0e38,
                                                    ALU.add, ALU.max, sm[:, q, 0, j:j + 1])
                last.then_inc(u_X, 1)
                dve.wait_ge(u_X, u + 1)
                if h % 2:
                    dve.tensor_scalar(sm[:, q, 0], sm[:, q, 0], -1.0, None, ALU.mult).then_inc(u_neg, 1)
                    dve.wait_ge(u_neg, g * (HEADS // 2) + h // 2 + 1)
                dve.scalar_tensor_tensor(sm[:, q, 1], sm[:, q, 0], SLOPE, sm[:, q, 0], ALU.mult,
                                         ALU.min if h % 2 else ALU.max).then_inc(u_mx, 1)
                dve.scalar_tensor_tensor(X_u[:, q], X_u[:, q], SLOPE, X_u[:, q], ALU.mult,
                                         ALU.max).then_inc(u_Y, 1)

            def row_sums(g, b, h):
                u = g * HEADS + h
                q = h % 2
                dve.wait_ge(u_E, u + 1)
                back(dve, u_P, u - 1)
                if h % 2 == 0:
                    dve.tensor_reduce(sm[:, q, 2], E_u[:, q], AX.X, ALU.add).then_inc(u_s, 1)
                    dve.wait_ge(u_s, g * (HEADS // 2) + h // 2 + 1)
                dve.reciprocal(sm[:, q, 3], sm[:, q, 2]).then_inc(u_r, 1)

            def to_out(g, b, h):
                if h == HEADS - 1:
                    dve.wait_ge(u_AV, g * HEADS + HEADS)
                    dve.wait_ge(e_hc, g + 1)
                    back(dve, e_th, g - 1)
                    dve.tensor_tensor(o_s[:, b], ps[:, 4 + b], hc_s[:, b], ALU.add).then_inc(e_o, 1)

            stats_e = ln_stats(E_PH, lambda g, b: dve.wait_ge(d_x3, g + 1))
            shift_e = ln_shift(E_PH)

            def split_rows(hi_sem, done, biased, rows_hi, rows_full, n, g):
                dve.wait_ge(biased, g + 1)
                dve.tensor_copy(rows_hi[0:n], rows_full[0:n]).then_inc(hi_sem, 1)
                dve.wait_ge(hi_sem, g + 1)
                dve.tensor_tensor(rows_hi[LOW:n], rows_full[LOW:n], rows_hi[LOW:n].bitcast(F32),
                                  ALU.subtract).then_inc(done, 1)

            def group(g, b):
                for h in range(HEADS):
                    units(g, b, h, [(2, row_sums), (0, mask_max), (6, to_out)])
                    if h == 1 and has(g + 1):
                        back(dve, u_S, g * HEADS)
                        split_rows(e_khi, e_K, e_kb, split[:, 1 - b, 2], flat(kf_s[:, 1 - b]), LOW + HEADS, g + 1)
                        split_rows(e_qhi, e_Q, e_qb, split[:, 1 - b, 3, 0:P], qf_s[:, 1 - b, 0:P], 2 * LOW, g + 1)
                    if h == 1 and has(g + 2):
                        stats_e(g + 2, b, 0)
                    if h == 3 and has(g + 2):
                        shift_e(g + 2, b, 0)
                    if h == 6 and has(g + 2):
                        dve.wait_ge(e_hhi, g + 3)
                        dve.tensor_tensor(split[:, b, 1], flat(heT_s[:, b]), split[:, b, 0].bitcast(F32),
                                          ALU.subtract).then_inc(e_split, 1)

            all_groups(dve, group)

        @block.scalar
        def _(act):
            for dst, src in WLOADS[11:]:
                act.dma_start(dst, src).then_inc(w_in, 16)

            def ln_apply(ph, dst, free, scale=None):
                def stage(g, b, _):
                    t = g + NG * ph
                    act.wait_ge(ln_nmr, t + 1)
                    free(g, b)
                    s = rstd[:, b] if scale is None else small[:, b, 7]
                    for j in range(GW):
                        last = act.activation(dst[:, b, j], x_all[:, g, j], ACT.Relu, bias=nmr[:, b, j:j + 1],
                                              scale=s[:, j:j + 1])
                    last.then_inc(ln_h, 1)
                return stage

            act.wait_ge(p_mm, 2)
            for l in range(STEPS):
                act.activation(gru_w[:, 0, l], ps[:, l, 0:3 * P], ACT.Copy).then_inc(p_ahi, 1)
            for k in range(2):
                act.activation(G[:, 0, 512 * k:512 * k + 512], ps[:, 6 + k], ACT.Copy).then_inc(p_ahi, 1)

            def keep_T(g, b, _):
                act.wait_ge(a_T, g + 1)
                back(act, a_proj, g - 1)
                act.activation(hT_s[:, b], ps[:, 0].rearrange("p (j e) -> p j e", e=P), ACT.Copy).then_inc(a_hT, 1)

            def keep_adjT(g, b, _):
                act.wait_ge(a_Ta, g + 1)
                back(act, a_agg, g - 1)
                act.activation(adjT_s[:, b], ps[:, 1].rearrange("p (j e) -> p j e", e=P), ACT.Copy).then_inc(a_adjT, 1)

            def exps(g, b, _):
                act.wait_ge(a_proj, g + 1)
                fe = ps[:, 2 + 4 * b:4 + 4 * b, :].rearrange("p k (j e) -> p k j e", e=256)
                act.activation(ef[:, g].rearrange("p (k j) -> p k j", j=2), fe[:, :, :, P], ACT.Exp,
                               bias=c0[:, 0:1])
                back(act, a_agg, g - 1)
                act.activation(Y_s[b][:, :, P].rearrange("p (k j) -> p k j", j=2), fe[:, :, :, P + 1], ACT.Exp,
                               bias=c0[:, 1:2]).then_inc(a_exp, 1)
                act.wait_ge(a_exp, g + 1)
                for j in range(GW):
                    last = act.activation(Y_s[b][:, j, 0:P], ps[:, 2 + 4 * b + j // 2, (j % 2) * 256:(j % 2) * 256 + P],
                                          ACT.Copy, scale=Y_s[b][:, j, P:P + 1])
                last.then_inc(a_Y, 1)

            sweep(act, [(0, keep_adjT), (1, keep_T), (0, exps), (3, ln_apply(A_PH, h_s, lambda g, b: back(act, a_T, g - 1)))])
            if upto < 2:
                return

            act.wait_ge(a_agg, NG)

            def keep_hT(g, b, _):
                act.wait_ge(b_T, g + 1)
                act.activation(hT_all[:, g], ps[:, b], ACT.Copy).then_inc(b_hT, 1)

            sweep(act, [(0, keep_hT), (2, ln_apply(B_PH, w1[6], lambda g, b: back(act, b_g, g - 1)))])

            def high_g(g, b, l):
                t = g + NG * l
                if l == 0:
                    act.wait_ge(b_gT, g + 1)
                else:
                    act.wait_ge(c_gk, t - NG + 1)
                back(act, c_z, t - 1)
                act.activation(split[:, b, 2], gT_all[:, g], ACT.Copy).then_inc(c_ghi, 1)

            def gates(g, b, l):
                t = g + NG * l
                act.wait_ge(c_r, t + 1)
                back(act, c_t1, t - 1)
                act.activation(w1[0][:, b].rearrange("p j e -> p (j e)"), ps[:, 0], ACT.Sigmoid,
                               bias=gate_b[:, 0:1]).then_inc(c_sr, 1)
                act.wait_ge(c_z, t + 1)
                back(act, c_zd, t - 1)
                act.activation(w1[1][:, b].rearrange("p j e -> p (j e)"), ps[:, 3], ACT.Sigmoid,
                               bias=gate_b[:, 1:2]).then_inc(c_sz, 1)
                act.wait_ge(c_t2, t + 1)
                back(act, c_h, t - 1)
                act.activation(w1[3][:, b], w1[2][:, b], ACT.Tanh, bias=gate_b[:, 2:3]).then_inc(c_n, 1)

            def keep_h(g, b, l):
                t = g + NG * l
                act.wait_ge(c_h, t + 1)
                act.activation(hT_all[:, g], w1[5][:, b].rearrange("p j e -> p (j e)"), ACT.Copy).then_inc(c_hk, 1)
                if l < STEPS - 1:
                    act.wait_ge(c_T, t + 1)
                    back(act, c_g, t - 1)
                    act.activation(w1[6][:, b].rearrange("p j e -> p (j e)"), ps[:, 4 + b], ACT.Copy).then_inc(c_nat, 1)

            def keep_g(g, b, l):
                if l == STEPS - 1:
                    return
                t = g + NG * l
                act.wait_ge(c_g, t + 1)
                act.activation(gT_all[:, g], ps[:, 6 + b], ACT.Copy).then_inc(c_gk, 1)

            sweep(act, [(1, high_g), (0, gates), (-1, keep_h), (-3, keep_g)], STEPS)
            if upto < 3:
                return

            act.wait_ge(c_x2, NG)

            def keep_HT(g, b, _):
                act.wait_ge(d_HT, g + 1)
                back(act, d_o, g - 1)
                act.activation(hT_s[:, b].rearrange("p j e -> p (j e)"), ps[:, 2 + b], ACT.Copy).then_inc(d_HTk, 1)

            def scale_o(g, b, _):
                act.wait_ge(d_o, g + 1)
                for j in range(GW):
                    last = act.activation(hT_all[:, g, j * P:(j + 1) * P], ps[:, 4 + b, j * P:(j + 1) * P], ACT.Copy,
                                          scale=deg[:, g, j:j + 1])
                last.then_inc(d_t, 1)

            sweep(act, [(-2, keep_HT), (-3, scale_o), (0, ln_apply(D_PH, h_s, lambda g, b: back(act, d_HT, g - 1), True))])
            if upto < 4:
                return

            for k in range(2):
                rows = slice(k * LOW, (k + 1) * LOW)
                pick = ident[rows, rows].rearrange("p (j h) -> p h j", h=HEADS).unsqueeze(3)
                act.activation(qsel[rows].rearrange("p (h j m) -> p h j m", h=HEADS, j=GW),
                               pick.to_broadcast([LOW, HEADS, GW, P]), ACT.Copy).then_inc(e_qsel, 1)

            def exponent(g, b, h):
                u = g * HEADS + h
                q = h % 2
                back(act, u_P, u - 1)
                if h % 2:
                    act.wait_ge(u_Y, u + 1)
                    for j in range(GW):
                        last = act.activation(E_u[:, q, j], X_u[:, q, j], ACT.Exp, bias=sm[:, q, 1, j:j + 1],
                                              accum_out=sm[:, q, 2, j:j + 1])
                    last.then_inc(u_E, 1)
                else:
                    act.wait_ge(u_Z, g * (HEADS // 2) + h // 2 + 1)
                    act.activation(E_u[:, q], Z_u[:, q], ACT.Exp).then_inc(u_E, 1)

            def keep_A(g, b, h):
                u = g * HEADS + h
                q = h % 2
                act.wait_ge(u_T, u + 1)
                back(act, u_AV, u - 3)
                act.activation(flat(A_u[:, h % 4]), ps[:, 2 + q], ACT.Copy).then_inc(u_A, 1)

            def tanh(g, b, h):
                if h == HEADS - 1:
                    act.wait_ge(e_o, g + 1)
                    back(act, e_sg, g - 1)
                    act.activation(t_s[:, b], o_s[:, b], ACT.Tanh, scale=0.5).then_inc(e_th, 1)

            def free_he(g, b):
                back(act, e_hc, g - 1)
                back(act, e_T, g - 1)
                act.wait_ge(d_T, NG)

            def keep_V(g, b, c):
                act.wait_ge(e_V, g * HEADS + c + 1)
                back(act, u_AV, (g - 1) * HEADS)
                act.activation(V[:, b, c // 2, (c % 2) * 512:(c % 2) * 512 + 512], ps[:, 7 - c % 2],
                               ACT.Copy).then_inc(e_Vk, 1)

            apply_e = ln_apply(E_PH, he_s, free_he)

            def group(g, b):
                for h in range(HEADS):
                    if h == 0 and has(g + 1):
                        act.wait_ge(e_k, g + 2)
                        back(act, e_K, g)
                        act.activation(flat(kf_s[:, 1 - b])[0:LOW + HEADS], ps[0:LOW + HEADS, 7], ACT.Identity,
                                       bias=ck[0:LOW + HEADS]).then_inc(e_kb, 1)
                        act.wait_ge(e_q, g + 2)
                        back(act, e_Q, g)
                        act.activation(qf_s[0:2 * LOW, 1 - b, 0:P], ps[0:2 * LOW, 6, 0:P], ACT.Identity,
                                       bias=cq[0:2 * LOW]).then_inc(e_qb, 1)
                    units(g, b, h, [(4, keep_A), (1, exponent), (6, tanh)])
                    value_chunk(g, b, h, keep_V)
                    if h == 3 and has(g + 2):
                        apply_e(g + 2, b, 0)
                    if h == 4 and has(g + 2):
                        act.wait_ge(e_T, g + 3)
                        back(act, e_split, g + 1)
                        back(act, e_q, g + 1)
                        act.activation(flat(heT_s[:, b]), ps[:, 6], ACT.Copy).then_inc(e_hT, 1)
                        back(act, e_V, HEADS * (g + 1))
                        act.wait_ge(e_hT, g + 3)
                        act.activation(split[:, b, 0], flat(heT_s[:, b]), ACT.Copy).then_inc(e_hhi, 1)

            all_groups(act, group)

        @block.tensor
        def _(pe):
            pe.wait_ge(w_in, 16 * len(WLOADS))
            pe.wait_ge(p_id, 1)
            for k, tile in enumerate(tiles):
                n = tile.shape[0]
                last = pe.transpose(ps[:, k // 4, (k % 4) * P:(k % 4) * P + n], tile, ident[0:n, 0:n])
                if k % 4 == 3 or k == NT - 1:
                    last.then_inc(p_T, 1)
            pe.wait_ge(p_bld, 1)
            pe.wait_ge(p_Tc, TB)

            def tT(k):
                return sT[:, k * P:(k + 1) * P]

            pe.matmul(ps[:, 5, 0:2], r_w0, r_a, start=True, stop=True)
            pe.matmul(ps[:, 5, 2:4], b0rep, r_a, start=True, stop=True)
            for h in range(HEADS):
                pe.matmul(ps[:, 5, 8 + 2 * h:10 + 2 * h], tT(T_FC + h), r_qk, start=True, stop=True)
            pe.matmul(ps[0:LOW + HEADS, 5, 32:33], fcbk[:, 0:LOW + HEADS], r_qk[:, 1:2], start=True, stop=True)
            pe.matmul(ps[0:2 * LOW, 5, 33:34], fcbq, r_qk[:, 0:1], start=True, stop=True)
            for h in range(HEADS):
                last = pe.matmul(ps[:, 5, 128:256], fcbrep[:, h], r_fp[:, h], start=(h == 0), stop=(h == HEADS - 1))
            last.then_inc(p_mm, 1)
            for l in range(STEPS):
                pe.matmul(ps[:, l, 0:3 * P], tT(T_GW + l), sT[:, T_WIH * P:(T_WIH + 3) * P], start=True, stop=True)
            for h in range(HEADS):
                last = pe.matmul(ps[:, 6 + h // 4, (h % 4) * P:(h % 4) * P + P], tT(T_FC + h), r_fp[:, h],
                                 start=True, stop=True)
            last.then_inc(p_mm, 1)
            pe.wait_ge(p_done, 1)
            pe.wait_ge(a_ycol, 1)

            def transposes(g, b, _):
                pe.wait_ge(ln_h, g + 1)
                back(pe, a_hT, g)
                for j in range(GW):
                    last = pe.transpose(ps[:, 0, j * P:(j + 1) * P], h_s[:, b, j], ident[:, :])
                last.then_inc(a_T, 1)

            def adj_transposes(g, q, _):
                pe.wait_ge(a_ld[q], (g - q) * 4 + 16)
                back(pe, a_adjT, g)
                for j in range(GW):
                    last = pe.transpose(ps[:, 1, j * P:(j + 1) * P], adj4[:, q, j], ident[:, :])
                last.then_inc(a_Ta, 1)

            def project(g, b, _):
                pe.wait_ge(a_hT, g + 1)
                back(pe, a_Y, g - 1)
                for j in range(GW):
                    o = (j % 2) * 256
                    last = pe.matmul(ps[:, 2 + 4 * b + j // 2, o:o + P + 2], hT_s[:, b, j], W0e[:, :], start=True, stop=True)
                last.then_inc(a_proj, 1)

            def aggregate(g, b, _):
                pe.wait_ge(a_Y, g + 1)
                pe.wait_ge(a_adjT, g + 1)
                back(pe, a_x1, g)
                for j in range(GW):
                    o = (j % 2) * 256
                    last = pe.matmul(ps[:, 4 + j // 2, o:o + P + 2], adjT_s[:, b, j], Y_s[b][:, j], start=True, stop=True)
                last.then_inc(a_agg, 1)

            sweep(pe, [(1, adj_transposes), (2, by_pairs(transposes)), (-1, by_pairs(aggregate)), (1, by_pairs(project))], ring=4)
            if upto < 2:
                return

            def b_trans(g, b, _):
                pe.wait_ge(ln_h, NG * B_PH + g + 1)
                back(pe, b_hT, g - 1)
                for j in range(GW):
                    last = pe.transpose(ps[:, b, j * P:(j + 1) * P], w1[6][:, b, j], ident[:, :])
                last.then_inc(b_T, 1)

            def b_agg(g, b, _):
                pe.wait_ge(a_edges, NG)
                back(pe, b_gT, g - 1)
                for j in range(GW):
                    last = pe.matmul(ps[:, 6 + b, j * P:(j + 1) * P], w1[6][:, b, j], edges[:, g, j], start=True, stop=True)
                last.then_inc(b_g, 1)

            sweep(pe, [(1, b_trans), (1, b_agg)])

            def three(bank, w, col, src, b, start, stop, l):
                hi, lo = gru_w[:, 0, w, col * P:(col + 1) * P], gru_w[:, 1, w, col * P:(col + 1) * P]
                pe.matmul(ps[:, bank], hi, split[:, b, src], start=start, stop=False)
                pe.matmul(ps[:, bank], lo, split[:, b, src], start=False, stop=False)
                return pe.matmul(ps[:, bank], hi, split[:, b, src + 1], start=False, stop=stop)

            def gate_products(g, b, l):
                t = g + NG * l
                pe.wait_ge(c_hsp, t + 1)
                back(pe, c_sr, t)
                if l == 0:
                    pe.wait_ge(b_hT, NG)
                three(0, STEPS, 0, 0, b, True, False, l)
                pe.wait_ge(c_glo, t + 1)
                three(0, l, 0, 2, b, False, True, l).then_inc(c_r, 1)
                back(pe, c_t1, t)
                three(1, STEPS, 2, 0, b, True, True, l).then_inc(c_hn, 1)
                back(pe, c_t2, t)
                three(2, l, 2, 2, b, True, True, l).then_inc(c_in, 1)
                back(pe, c_sz, t)
                three(3, STEPS, 1, 0, b, True, False, l)
                three(3, l, 1, 2, b, False, True, l).then_inc(c_z, 1)

            def c_trans(g, b, l):
                t = g + NG * l
                pe.wait_ge(c_h, t + 1)
                if l < STEPS - 1:
                    back(pe, c_nat, t - 1)
                else:
                    pe.wait_ge(c_nat, NG * (STEPS - 1))
                    back(pe, c_x2, g - 1)
                for j in range(GW):
                    last = pe.transpose(ps[:, 4 + b, j * P:(j + 1) * P], w1[5][:, b, j], ident[:, :])
                last.then_inc(c_T, 1)

            def c_agg(g, b, l):
                if l == STEPS - 1:
                    return
                t = g + NG * l
                pe.wait_ge(c_nat, t + 1)
                if l == 0:
                    pe.wait_ge(b_gT, NG)
                back(pe, c_gk, t - 1)
                for j in range(GW):
                    last = pe.matmul(ps[:, 6 + b, j * P:(j + 1) * P], w1[6][:, b, j], edges[:, g, j], start=True, stop=True)
                last.then_inc(c_g, 1)

            sweep(pe, [(0, gate_products), (-1, c_trans), (-2, c_agg)], STEPS)
            if upto < 3:
                return

            pe.wait_ge(c_x2, NG)

            def d_trans(g, q, _):
                b = q % 2
                pe.wait_ge(d_ld[q], (g - q) * 4 + 16)
                back(pe, d_adjT, g - 1)
                for j in range(GW):
                    last = pe.transpose(ps[:, b, j * P:(j + 1) * P], adj4[:, q, j], ident[:, :])
                last.then_inc(d_T, 1)

            def d_agg(g, b, _):
                pe.wait_ge(d_adjT, g + 1)
                pe.wait_ge(ln_h, NG * D_PH + g + 1)
                back(pe, d_HTk, g - 1)
                for j in range(GW):
                    last = pe.matmul(ps[:, 2 + b, j * P:(j + 1) * P], h_s[:, b, j], adjT_s[:, b, j], start=True, stop=True)
                last.then_inc(d_HT, 1)

            def d_project(g, b, _):
                pe.wait_ge(d_HTk, g + 1)
                back(pe, d_t, g - 1)
                for j in range(GW):
                    last = pe.matmul(ps[:, 4 + b, j * P:(j + 1) * P], hT_s[:, b, j], W2T[:, :], start=True, stop=True)
                last.then_inc(d_o, 1)

            sweep(pe, [(1, d_trans), (-1, by_pairs(d_agg)), (-2, by_pairs(d_project))], ring=4)
            if upto < 4:
                return

            pe.wait_ge(d_x3, NG)

            def logits(g, b, h):
                u = g * HEADS + h
                q = h % 2
                pe.wait_ge(e_qsel, 2)
                pe.wait_ge(e_K, g + 1)
                pe.wait_ge(e_Q, g + 1)
                back(pe, u_X, u - 1)
                pe.matmul(ps[:, q], split[0:2 * LOW, b, 3, 0:P], qsel[:, h * ROWS:(h + 1) * ROWS], start=True, stop=False)
                pe.matmul(ps[:, q], selk[:, h], split[0:LOW + HEADS, b, 2], start=False, stop=True).then_inc(u_S, 1)

            def probs_T(g, b, h):
                u = g * HEADS + h
                q = h % 2
                pe.wait_ge(u_P, u + 1)
                back(pe, u_A, u - 1)
                for j in range(GW):
                    last = pe.transpose(ps[:, 2 + q, j * P:(j + 1) * P], P_u[:, h % 4, j], ident[:, :])
                last.then_inc(u_T, 1)

            def attend(g, b, h):
                u = g * HEADS + h
                q = h % 2
                pe.wait_ge(u_A, u + 1)
                pe.wait_ge(e_Vk, (g + 1) * HEADS)
                if h == 0:
                    back(pe, e_o, g - 1)
                for j in range(GW):
                    last = pe.matmul(ps[:, 4 + b, j * P:(j + 1) * P], A_u[:, h % 4, j], V[:, b, j, h * P:(h + 1) * P],
                                     start=(h == 0 and j == 0), stop=(h == HEADS - 1), skip_group_check=True)
                last.then_inc(u_AV, 1)

            def values(g, b, c):
                pe.wait_ge(e_split, g + 1)
                back(pe, e_Vk, g * HEADS + c - 1)
                j, bank, cols = c // 2, 7 - c % 2, slice((c % 2) * 512, (c % 2) * 512 + 512)
                hi, lo = (split[:, b, k, j * P:(j + 1) * P] for k in range(2))
                pe.matmul(ps[:, bank], hi, G[:, 0, cols], start=True, stop=False)
                pe.matmul(ps[:, bank], lo, G[:, 0, cols], start=False, stop=False)
                pe.matmul(ps[:, bank], hi, G[:, 1, cols], start=False, stop=True).then_inc(e_V, 1)

            def group(g, b):
                for h in range(HEADS):
                    units(g, b, h, [(0, logits), (4, probs_T), (5, attend)])
                    if h == 0 and has(g + 1):
                        pe.wait_ge(e_hT, g + 2)
                        back(pe, e_Vk, g * HEADS + 3)
                        pe.matmul(ps[0:LOW + HEADS, 7], Wk[:, :], flat(heT_s[:, 1 - b]), start=True, stop=True).then_inc(e_k, 1)
                        back(pe, e_Vk, g * HEADS + 4)
                        for j in range(GW):
                            last = pe.matmul(ps[0:2 * LOW, 6, 0:P], Wq[:, j], heT_s[:, 1 - b, j], start=(j == 0), stop=(j == GW - 1))
                        last.then_inc(e_q, 1)
                    if h == 0 and has(g + 1):
                        pe.wait_ge(e_kb, g + 2)
                    if h == 1 and has(g + 1):
                        pe.wait_ge(e_qb, g + 2)
                    if h == 5 and has(g + 2):
                        pe.wait_ge(e_hT, g + 3)
                    value_chunk(g, b, h, values)
                    if h == 4 and has(g + 2):
                        pe.wait_ge(ln_h, NG * E_PH + (g + 2) + 1)
                        back(pe, e_Vk, HEADS * (g + 1))
                        for j in range(GW):
                            last = pe.transpose(ps[:, 6, j * P:(j + 1) * P], he_s[:, b, j], ident[:, :])
                        last.then_inc(e_T, 1)

            all_groups(pe, group)


_INS = ["x", "adj", "nodemask", "L0_gnn_W_w", "L0_gnn_W_b", "L0_gnn_a_w", "L0_gnn_a_b", "L1_gnn_weight", "L1_gnn_w_ih",
        "L1_gnn_w_hh", "L1_gnn_b_ih", "L1_gnn_b_hh", "L2_gnn_W", "L2_gnn_b", "L3_gnn_fc_w", "L3_gnn_fc_b", "L3_gnn_q_w",
        "L3_gnn_q_b", "L3_gnn_k_w", "L3_gnn_k_b", "L3_gnn_fp_w", "L3_gnn_fp_b"]


def kernel(**inputs):
    import numpy as _np
    import concourse.bacc as _bacc
    from concourse import mybir as _mybir
    from concourse.bass_utils import run_bass_kernel_spmd as _run

    nc = _bacc.Bacc("TRN2", target_bir_lowering=False, num_devices=1)
    arrays, args = {}, []
    for name in _INS:
        a = _np.ascontiguousarray(inputs[name])
        arrays[f"in_{name}"] = a
        args.append(nc.dram_tensor(f"in_{name}", a.shape, _mybir.dt.from_np(a.dtype), kind="ExternalInput").ap())
    o = nc.dram_tensor("out_x", (GRAPHS, P, P), F32, kind="ExternalOutput").ap()
    build(nc, *args, o)
    r = _run(nc, [arrays], core_ids=[0])
    return r.results[0]["out_x"]
```

```python
from contextlib import ExitStack

import concourse.bass as bass
from concourse import mybir

F32 = mybir.dt.float32
F32R = mybir.dt.float32r
ALU = mybir.AluOpType
ACT = mybir.ActivationFunctionType
AX = mybir.AxisListType

P = 128
GRAPHS = 64
GW = 4
NG = GRAPHS // GW
HEADS = 8
STEPS = 5
EPS = 1e-5
NEG = -1e9
SLOPE = 0.01
ROWS = GW * P
LOW = 32
QK = 2 * LOW
VALUES_FROM = 5
KQ = 3 * LOW + HEADS
A_PH, B_PH, D_PH, E_PH = range(4)


def by_pairs(stage):
    return lambda g, place, block: stage(g, place % 2, block)


def back(eng, sem, value):
    if isinstance(value, int) and value <= 0:
        return
    eng.wait_ge(sem, value)


def alone(eng, met):
    eng.sem_inc(met, 1)


def sweep(eng, *segments, ring=2):
    n, spans, start = NG, [], 0
    for blocks, stages in segments:
        spans.append((start, start + int(blocks * n), stages))
        start += int(blocks * n)
    lead = [max([0] + [o for o, _ in stages]) for _, _, stages in spans] + [0]
    lag = [max([0] + [-o for o, _ in stages]) for _, _, stages in spans] + [0]

    def written_out(i):
        for begin, end, stages in spans:
            for o, stage in stages:
                t = i + o
                if begin <= t < end:
                    stage((t - begin) % n, t % ring, (t - begin) // n)

    for i in range(-lead[0], 0):
        written_out(i)
    for k, (begin, end, stages) in enumerate(spans):
        for block in range(-(-(end - begin) // n)):
            at = begin + block * n
            if end - at < n:
                for i in range(at, end):
                    written_out(i)
                continue
            into = lag[k - 1] if block == 0 and k else 0
            out_of = lead[k + 1] if at + n == end else 0
            first = -(-max(2 + lag[k], into) // ring) * ring
            last = (n - max(lead[k], out_of)) // ring * ring
            for i in range(at, at + first):
                written_out(i)
            with eng.Fori(first // ring, last // ring) as turn:
                for place in range(ring):
                    for o, stage in stages:
                        stage(turn * ring + (place + o), (place + o) % ring, block)
            for i in range(at + last, at + n):
                written_out(i)
    for i in range(start, start + max(lag)):
        written_out(i)


def build(nc, x_in, adj_in, mask_in, w0_in, b0_in, a_in, ab_in, gw_in, wih_in, whh_in, bih_in, bhh_in,
          w2_in, b2_in, fc_in, fcb_in, qw_in, qb_in, kw_in, kb_in, fp_in, fpb_in, out):
    with ExitStack() as ctx:
        def sb(name, shape, dt=F32):
            return ctx.enter_context(nc.sbuf_tensor(name, shape, dt))

        def sem(name):
            return ctx.enter_context(nc.semaphore(name))

        x_all = sb("x_all", [P, NG, GW, P])
        ident = sb("ident", [P, P])
        half = sb("half", [P, GW])
        edges = sb("edges", [P, NG, GW, P])
        hT_all = sb("hT_all", [P, NG, ROWS])
        gT_all = sb("gT_all", [P, NG, ROWS])
        W0e = sb("W0e", [P, P + 2])
        c0 = sb("c0", [P, 2])
        b0row = sb("b0row", [P, P])
        ab = sb("ab", [P, 1])
        gru_w = sb("gru_w", [P, 2, STEPS + 1, 3 * P], F32R)
        gate_b = sb("gate_b", [P, 4])
        maskT = sb("maskT", [P, GRAPHS])
        W2T = sb("W2T", [P, P])
        b2row = sb("b2row", [P, P])
        deg = sb("deg", [P, NG, GW])
        G = sb("G", [P, 2, HEADS * P], F32R)
        Wkq = sb("Wkq", [P, KQ])
        ckq = sb("ckq", [P, 1])
        ce = sb("ce", [P, P])
        selk = sb("selk", [LOW + HEADS, HEADS, P], F32R)
        pick = sb("pick", [2 * LOW, LOW], F32R)
        bn = sb("bn", [P, 2, GW, 6])
        mv = sb("mv", [P, 2, GW, 2])
        ve = sb("ve", [P, 2, GW])
        rstd = sb("rstd", [P, 2, GW])
        nmr = sb("nmr", [P, 2, GW])
        work = [sb(f"work{i}", [P, 2, GW, P]) for i in range(7)]
        split = sb("split", [P, 2, 4, ROWS], F32R)
        small = sb("small", [P, 2, 8, GW])
        ps = ctx.enter_context(nc.psum_tensor("ps", [P, 8, 512], F32))

        st = hT_all[:, :, :].rearrange("p a b -> p (a b)")
        sT = gT_all[:, :, :].rearrange("p a b -> p (a b)")
        r_w0, r_w2, r_mask = st[:, 0:128], st[:, 128:256], st[0:GRAPHS, 256:384]
        r_gw = st[:, 384:1024].rearrange("p (l e) -> p l e", e=P)
        r_wih = st[:, 1024:1408].rearrange("p (l e) -> p l e", e=P)
        r_whh = st[:, 1408:1792].rearrange("p (l e) -> p l e", e=P)
        r_fc = st[:, 1792:2816].rearrange("p (l e) -> p l e", e=P)
        r_fp = st[:, 6272:7296].rearrange("p (l e) -> p l e", e=P)
        r_vec = st[0:19, 3712:3840]
        vec0 = (9 + STEPS + HEADS) * P
        r_a, r_b0 = sT[:, vec0:vec0 + 2], sT[:, vec0 + 2:vec0 + 3]
        r_bih, r_bhh = sT[:, vec0 + 3:vec0 + 6], sT[:, vec0 + 6:vec0 + 9]
        r_fcb, r_qk = sT[:, vec0 + 9:vec0 + 17], sT[:, vec0 + 17:vec0 + 19]
        adj4 = sT[:, 8 * ROWS:12 * ROWS].rearrange("p (b j e) -> p b j e", b=4, j=GW)
        ef = sT[:, (NG - 1) * ROWS:(NG - 1) * ROWS + NG * GW].rearrange("p (g j) -> p g j", g=NG)
        r_qb, r_kb = st[:, 3859:3860], st[:, 3860:3861]
        b0rep = st[:, 3968:4096]
        fcbkq = st[:, 4096:4096 + KQ]
        fcbrep = st[:, 4224:4224 + 1024].rearrange("p (h e) -> p h e", e=P)
        tiles = [r_w0, r_w2, r_mask, r_whh[:, 0], r_whh[:, 1], r_whh[:, 2], r_wih[:, 0], r_wih[:, 1], r_wih[:, 2]]
        tiles += [r_gw[:, l] for l in range(STEPS)] + [r_fc[:, h] for h in range(HEADS)] + [r_vec]
        T_WHH, T_WIH, T_GW, T_FC = 3, 6, 9, 9 + STEPS
        NT = len(tiles)
        TB = -(-NT // 4)
        assert TB <= 6

        w_first, w_gru, w_fp, w_small = sem("first_weights_in"), sem("gru_fc_in"), sem("fp_in"), sem("small_weights_in")
        p_id0, p_id = sem("prep_ident_zero"), sem("prep_ident")
        p_T, p_Tc, p_TcA, p_bld = (sem("prep_transposed"), sem("prep_kept_by_vector"), sem("prep_kept_by_scalar"),
                                  sem("prep_built"))
        p_mm, p_hi, p_done = sem("prep_products"), sem("prep_high"), sem("prep_done")
        p_ahi = sem("prep_act_high")
        dve_met, pool_met, sp_met = sem("vector_waits_met"), sem("gpsimd_waits_met"), sem("sync_waits_met")
        ln_bn, ln_mv, ln_ve = sem("ln_bn"), sem("ln_mv"), sem("ln_ve")
        ln_rstd, ln_nmr, ln_h = sem("ln_rstd"), sem("ln_nmr"), sem("ln_h")
        x_ld = [sem(f"x_landed{i}") for i in range(2)]
        a_ld = [sem(f"adj_landed{i}") for i in range(4)]
        a_T, a_Ta, a_adjT, a_hT = sem("a_h_transposed"), sem("a_adj_transposed"), sem("a_adjT_kept"), sem("a_hT_kept")
        a_proj, a_exp, a_Y, a_agg = sem("a_projected"), sem("a_exps"), sem("a_Y"), sem("a_aggregated")
        a_edges, a_xb, a_s1, a_s2, a_s3 = sem("a_edges"), sem("a_xb"), sem("a_den"), sem("a_rden"), sem("a_scale")
        a_x1 = sem("a_x1")
        a_ycol = sem("a_ycol")
        b_g, b_gT = sem("b_aggregated"), sem("b_gT_kept")
        c_hhi, c_hsp, c_ghi, c_glo = sem("c_h_high"), sem("c_h_split"), sem("c_g_high"), sem("c_g_low")
        c_r, c_hn, c_in, c_z = sem("c_r_ready"), sem("c_hn_ready"), sem("c_in_ready"), sem("c_z_ready")
        c_sr, c_sz, c_t1, c_t2, c_n = sem("c_r"), sem("c_z"), sem("c_t1"), sem("c_t2"), sem("c_n")
        c_d, c_zd, c_h = sem("c_h_minus_n"), sem("c_z_times"), sem("c_h_new")
        c_hk, c_T, c_nat, c_g, c_gk = sem("c_h_kept"), sem("c_transposed"), sem("c_nat"), sem("c_aggregated"), sem("c_g_kept")
        c_x2 = sem("c_x2")
        d_ld = [sem(f"d_adj_landed{i}") for i in range(2)]
        d_pow, d_dscale, d_T, d_adjT = sem("d_pow"), sem("d_scale"), sem("d_transposed"), sem("d_adjT")
        d_HT, d_HTk, d_o, d_t, d_t1, d_x3 = (sem("d_HT"), sem("d_HT_kept"), sem("d_out"), sem("d_scaled"),
                                             sem("d_biased"), sem("d_x3"))
        e_ld = [sem(f"e_adj_landed{i}") for i in range(2)]
        e_T, e_hT, e_hhi, e_split = sem("e_transposed"), sem("e_hT_kept"), sem("e_h_high"), sem("e_h_split")
        e_k, e_kb, e_khi, e_K = sem("e_k"), sem("e_k_biased"), sem("e_k_high"), sem("e_K_rows")
        e_ql = [sem(f"e_q_landed{i}") for i in range(2)]
        e_qhi, e_Q = sem("e_q_high"), sem("e_Q_rows")
        e_V, e_Vk, e_M, e_hc = sem("e_V"), sem("e_V_kept"), sem("e_M"), sem("e_hc")
        e_o, e_th, e_sg, e_x4 = sem("e_o"), sem("e_tanh"), sem("e_sigmoid"), sem("e_x4")
        u_neg = sem("u_negated")
        u_S, u_X, u_Y, u_Z, u_E = sem("u_S"), sem("u_X"), sem("u_leaky"), sem("u_shifted"), sem("u_exp")
        u_s, u_r, u_P, u_T, u_A, u_AV = sem("u_sum"), sem("u_rsum"), sem("u_probs"), sem("u_T"), sem("u_A_kept"), sem("u_AV")
        o_st = sem("out_stored")

        block = ctx.enter_context(nc.Block())

        def bcast(ap, n=GW):
            return ap.unsqueeze(1).to_broadcast([ap.shape[0], n, ap.shape[1]])

        def along(ap, n=P):
            return ap.unsqueeze(2).to_broadcast([ap.shape[0], ap.shape[1], n])

        W_FIRST = [(r_w0, w0_in), (r_w2, w2_in), (r_mask, mask_in),
                   (r_whh, whh_in.rearrange("(k r) d -> r k d", r=P)), (r_wih, wih_in.rearrange("(k r) d -> r k d", r=P))]
        W_ROWS = [(r_vec[0:2], a_in.rearrange("(t e) -> t e", e=P)), (r_vec[2:3], b0_in.rearrange("(t e) -> t e", e=P)),
                  (r_vec[3:6], bih_in.rearrange("(t e) -> t e", e=P)), (r_vec[6:9], bhh_in.rearrange("(t e) -> t e", e=P)),
                  (r_vec[9:17], fcb_in.rearrange("(t e) -> t e", e=P)), (r_vec[17:18], qw_in.rearrange("e t -> t e")),
                  (r_vec[18:19], kw_in.rearrange("e t -> t e"))]
        W_GRU = [(r_gw, gw_in.rearrange("l d e -> d l e")), (r_fc, fc_in.rearrange("d (h e) -> d h e", e=P))]
        W_FP = (r_fp, fp_in.rearrange("(h c) e -> c h e", c=P))
        W_SMALL = [(r_qb, qb_in.partition_broadcast(P)), (r_kb, kb_in.partition_broadcast(P)),
                   (ab[:, :], ab_in.partition_broadcast(P)), (b0row[:, :], b0_in.partition_broadcast(P)),
                   (b2row[:, :], b2_in.partition_broadcast(P)), (ce[:, :], fpb_in.partition_broadcast(P))]

        x_dram = x_in.rearrange("(g j) n d -> n g j d", j=GW)
        adj_dram = adj_in.rearrange("(g j) n m -> n g j m", j=GW)
        out_dram = out.rearrange("(g j) n d -> n g j d", j=GW)
        adj_s, h_s, hT_s, adjT_s, xb_s = work[0], work[1], work[2], work[3], work[4]
        gate_r, gate_z, pre_n, cand_n, diff, new_hT, new_h = work
        Y_s = [work[k][:, :, :, :].rearrange("p b j e -> p (b j e)")[:, 0:GW * (P + 2)]
               .rearrange("p (j e) -> p j e", e=P + 2) for k in (5, 6)]

        V = st.rearrange("p (b j c) -> p b j c", b=2, j=GW)
        unit = edges[:, :, :, :].rearrange("p (k b) j e -> p k b j e", b=2)
        X_u, E_u, P_u, A_u = (unit[:, k:k + 2].rearrange("p k b j e -> p (k b) j e") for k in (0, 2, 4, 6))
        he_s, heT_s, M_s, kf_s = work[1], work[2], work[3], work[4]
        spare = gT_all[:, :, :].rearrange("p (k b) r -> p k b r", b=2)
        hc_s, o_s, t_s, g_s, qf_s = (spare[:, k] for k in range(5))

        hd_s, HTd_s = work[6], work[5]
        adjTd_s = sT[:, 0:2 * ROWS].rearrange("p (b j e) -> p b j e", b=2, j=GW)

        def sm(h, k):
            return small[:, h % 2, 4 * ((h // 2) % 2) + k]

        def flat(ap):
            return ap.rearrange("p j e -> p (j e)")

        def units(g, b, h, stages):
            for lag, stage in stages:
                if lag > h:
                    if not (isinstance(g, int) and g <= 0):
                        stage(g - 1, 1 - b, h - lag + HEADS)
                elif not (isinstance(g, int) and not 0 <= g < NG):
                    stage(g, b, h - lag)

        def has(g):
            return not isinstance(g, int) or 0 <= g < NG

        def value_chunk(g, b, h, stage, lag=0):
            c = h - lag - VALUES_FROM
            g, b, c = (g + 1, 1 - b, c) if c >= 0 else (g, b, c + HEADS)
            if has(g):
                stage(g, b, c)

        def ahead(g):
            return not isinstance(g, int) or 0 <= g < NG - 2

        def all_groups(eng, group):
            for g in range(-1, 4):
                group(g, g % 2)
            with eng.Fori(2, NG // 2 - 1) as pair:
                for b in range(2):
                    group(pair * 2 + b, b)
            for g in (NG - 2, NG - 1, NG):
                group(g, g % 2)

        @block.sync
        def _(sp):
            for g in range(2):
                sp.dma_start(x_all[:, g], x_dram[:, g]).then_inc(x_ld[g], 16)
            for dst, src in W_FIRST:
                sp.dma_start(dst, src).then_inc(w_first, 16)
            for dst, src in W_GRU:
                sp.dma_start(dst, src).then_inc(w_gru, 16)

            def load_x(g, b, _):
                if isinstance(g, int) and g < 2:
                    return
                back(sp, x_ld[b], (g - b) * 8)
                sp.dma_start(x_all[:, g], x_dram[:, g]).then_inc(x_ld[b], 16)

            def load_adj(g, q, _):
                back(sp, a_edges, g - 3)
                back(sp, a_Ta, g - 3)
                sp.dma_start(adj4[:, q], adj_dram[:, g]).then_inc(a_ld[q], 16)

            sweep(sp, (1, [(4, by_pairs(load_x)), (2, load_adj)]), ring=4)

            sp.wait_ge(c_glo, NG * (STEPS - 1) + 10)

            def load_adj2(g, b, _):
                back(sp, d_T, g - 1)
                sp.dma_start(adj4[:, b], adj_dram[:, g]).then_inc(d_ld[b], 16)

            sweep(sp, (1, [(0, load_adj2)]))

            sp.wait_ge(d_T, NG)

            def load_adj3(g, b, _):
                back(sp, e_M, g - 1)
                sp.dma_start(adj_s[:, b], adj_dram[:, g]).then_inc(e_ld[b], 16)

            def place_q(g, b, _):
                sp.wait_ge(e_kb, g + 1)
                alone(sp, sp_met)
                back(sp, e_Q, g - 1)
                for k in range(2):
                    sp.dma_start(qf_s[k * LOW:(k + 1) * LOW, b, 0:P],
                                 flat(kf_s[:, b])[QK + k * LOW:QK + k * LOW + HEADS]).then_inc(e_ql[b], 16)

            def store(g, b, _):
                sp.wait_ge(e_x4, g + 1)
                sp.dma_start(out_dram[:, g], x_all[:, g]).then_inc(o_st, 16)

            sweep(sp, (1, [(1, place_q), (-2, store), (3, load_adj3)]))
            sp.wait_ge(o_st, 16 * NG)

        @block.gpsimd
        def _(pool):
            pool.memset(ident[:, :], 0.0).then_inc(p_id0, 1)
            pool.memset(half[:, :], -0.5)
            pool.memset(fcbkq, 0.0)
            pool.memset(ckq[:, :], 0.0)
            pool.memset(Wkq[:, :], 0.0).then_inc(p_id0, 1)
            pool.wait_ge(p_id0, 2)
            pool.affine_select(out=ident[:, :], in_=ident[:, :], compare_op=ALU.not_equal, fill=1.0, base=0,
                               pattern=[[-1, P]], channel_multiplier=1).then_inc(p_id, 1)
            for dst, src in W_SMALL:
                pool.dma_start(dst, src).then_inc(w_small, 16)

            def ln_pow(ph):
                def stage(g, b, _):
                    t = g + NG * ph
                    pool.wait_ge(ln_ve, t + 1)
                    back(pool, ln_h, t - 1)
                    pool.tensor_tensor(rstd[:, b], ve[:, b], half[:, :], ALU.pow).then_inc(ln_rstd, 1)
                return stage

            def x_plus_b(g, b, _):
                pool.wait_ge(w_small, 16 * len(W_SMALL))
                pool.wait_ge(x_ld[b], (g - b) * 8 + 16)
                back(pool, a_x1, g - 1)
                pool.tensor_tensor(xb_s[:, b], x_all[:, g], bcast(b0row[:, :]), ALU.add).then_inc(a_xb, 1)

            def deg_pow(g, b, _):
                pool.wait_ge(a_s3, g * 2 + 1)
                pool.tensor_tensor(deg[:, g], deg[:, g], half[:, :], ALU.pow).then_inc(d_pow, 1)

            sweep(pool, (1, [(-1, x_plus_b), (4, ln_pow(A_PH)), (-3, deg_pow)]), (1, [(4, ln_pow(B_PH))]))

            def h_minus_n(g, b, l):
                t = g + NG * l
                pool.wait_ge(c_n, t + 1)
                back(pool, c_h, t - 1)
                pool.tensor_tensor(flat(diff[:, b]), hT_all[:, g],
                                   flat(cand_n[:, b]), ALU.subtract).then_inc(c_d, 1)
                pool.wait_ge(c_d, t + 1)
                pool.wait_ge(c_sz, t + 1)
                pool.tensor_tensor(diff[:, b], diff[:, b], gate_z[:, b], ALU.mult).then_inc(c_zd, 1)

            def add_b2(g, b, _):
                pool.wait_ge(d_t, g + 1)
                t = hT_all[:, g].rearrange("p (j e) -> p j e", e=P)
                pool.tensor_tensor(t, t, bcast(b2row[:, :]), ALU.add).then_inc(d_t1, 1)

            sweep(pool, (STEPS, [(0, h_minus_n)]), (1, [(-4, add_b2), (2, ln_pow(D_PH))]), (2 / NG, [(2, ln_pow(E_PH))]))
            pool.wait_ge(d_HT, NG)

            def shift(g, b, h):
                if h % 2:
                    return
                u = g * HEADS + h
                pool.wait_ge(u_Y, u + 1)
                pool.tensor_tensor(X_u[:, h % 4], X_u[:, h % 4], along(sm(h, 1)), ALU.subtract).then_inc(u_Z, 1)

            def normalize(g, b, h):
                u = g * HEADS + h
                pool.wait_ge(u_r, u + 1)
                back(pool, u_T, u - 3)
                pool.tensor_tensor(P_u[:, h % 4], E_u[:, h % 4], along(sm(h, 3)), ALU.mult).then_inc(u_P, 1)

            def add_to_x(g, b):
                pool.wait_ge(e_th, g + 1)
                alone(pool, pool_met)
                pool.tensor_scalar(g_s[:, b], t_s[:, b], 0.5, 0.5, ALU.mult, ALU.add).then_inc(e_sg, 1)
                pool.wait_ge(e_sg, g + 1)
                pool.tensor_tensor(x_all[:, g], g_s[:, b].rearrange("p (j e) -> p j e", e=P), x_all[:, g],
                                   ALU.add).then_inc(e_x4, 1)

            ln_pow_e = ln_pow(E_PH)

            def group(g, b):
                for h in range(HEADS):
                    units(g, b, h, [(1, shift), (3, normalize)])
                    if h == 0 and has(g):
                        back(pool, e_o, g - 1)
                        pool.wait_ge(ln_h, NG * E_PH + g + 1)
                        pool.tensor_tensor(hc_s[:, b].rearrange("p (j e) -> p j e", e=P), he_s[:, b],
                                           bcast(ce[:, :]), ALU.add).then_inc(e_hc, 1)
                    if h == 2 and ahead(g):
                        ln_pow_e(g + 2, b, 0)
                    if h == 2 and has(g + 1):
                        pool.wait_ge(e_hhi, g + 2)
                        pool.tensor_tensor(split[:, 1 - b, 1], flat(heT_s[:, 1 - b]), split[:, 1 - b, 0].bitcast(F32),
                                           ALU.subtract).then_inc(e_split, 1)
                    if h == 4 and has(g - 2):
                        add_to_x(g - 2, b)
                    if h == 6 and has(g + 1):
                        pool.wait_ge(e_ld[1 - b], (g + 1 - (1 - b)) * 8 + 16)
                        back(pool, u_X, g * HEADS)
                        alone(pool, pool_met)
                        pool.tensor_scalar(M_s[:, 1 - b], adj_s[:, 1 - b], -1.0, -NEG, ALU.add,
                                           ALU.mult).then_inc(e_M, 1)
                    if h == 7 and isinstance(g, int) and g == NG:
                        add_to_x(NG - 1, 1 - b)

            all_groups(pool, group)

        @block.vector
        def _(dve):
            def ln_stats(ph, ready):
                def stage(g, b, _):
                    t = g + NG * ph
                    ready(g, b)
                    for j in range(GW):
                        last = dve.bn_stats(bn[:, b, j], x_all[:, g, j])
                    last.then_inc(ln_bn, 1)
                    dve.wait_ge(ln_bn, t + 1)
                    back(dve, ln_nmr, t - 1)
                    alone(dve, dve_met)
                    for j in range(GW):
                        last = dve.bn_aggr(mv[:, b, j], bn[:, b, j])
                    last.then_inc(ln_mv, 1)
                    dve.wait_ge(ln_mv, t + 1)
                    back(dve, ln_rstd, t - 1)
                    dve.tensor_scalar(ve[:, b], mv[:, b, :, 1], EPS, None, ALU.add).then_inc(ln_ve, 1)
                return stage

            def ln_shift(ph, gcn=False):
                def stage(g, b, _):
                    t = g + NG * ph
                    dve.wait_ge(ln_rstd, t + 1)
                    back(dve, ln_h, t - 1)
                    if gcn:
                        dve.wait_ge(d_pow, g + 1)
                        dve.tensor_tensor(small[:, b, 7], rstd[:, b], deg[:, g], ALU.mult).then_inc(d_dscale, 1)
                        dve.wait_ge(d_dscale, g + 1)
                        dve.scalar_tensor_tensor(nmr[:, b], mv[:, b, :, 0], -1.0, small[:, b, 7], ALU.mult,
                                                 ALU.mult).then_inc(ln_nmr, 1)
                    else:
                        dve.scalar_tensor_tensor(nmr[:, b], mv[:, b, :, 0], -1.0, rstd[:, b], ALU.mult,
                                                 ALU.mult).then_inc(ln_nmr, 1)
                return stage

            dve.wait_ge(p_id0, 2)
            dve.wait_ge(p_id, 1)
            dve.tensor_copy(selk[0:LOW], along(ident[0:LOW, 0:HEADS]))
            for k in range(2):
                dve.tensor_copy(pick[k * LOW:(k + 1) * LOW], ident[k * LOW:(k + 1) * LOW, k * LOW:(k + 1) * LOW])
            dve.tensor_copy(selk[LOW:LOW + HEADS], along(ident[LOW:LOW + HEADS, LOW:LOW + HEADS]))

            def prepare(g, q, _):
                if not isinstance(g, int) or g > 0:
                    return
                for k in range(TB):
                    n = min(4, NT - 4 * k) * P
                    if k % 2:
                        continue
                    dve.wait_ge(p_T, k + 1)
                    if k == 0:
                        dve.tensor_copy(sT[:, 0:256], ps[:, 0, 0:256])
                        dve.tensor_copy(maskT[:, :], ps[:, 0, 256:256 + GRAPHS])
                        dve.tensor_copy(sT[:, 384:512], ps[:, 0, 384:512]).then_inc(p_Tc, 1)
                    else:
                        dve.tensor_copy(sT[:, 512 * k:512 * k + n], ps[:, k, 0:n]).then_inc(p_Tc, 1)
                dve.wait_ge(p_Tc, TB // 2)
                dve.wait_ge(p_TcA, TB // 2)
                dve.tensor_copy(b0rep, r_b0.to_broadcast([P, P]))
                dve.tensor_copy(fcbrep, along(r_fcb))
                for k in range(4):
                    dve.tensor_copy(fcbkq[:, k * LOW:k * LOW + HEADS], r_fcb)
                dve.tensor_copy(gate_b[:, 2:3], r_bih[:, 2:3])
                dve.tensor_copy(gate_b[:, 3:4], r_bhh[:, 2:3])
                dve.tensor_tensor(gate_b[:, 0:2], r_bih[:, 0:2], r_bhh[:, 0:2], ALU.add).then_inc(p_bld, 1)
                dve.tensor_copy(W0e[:, 0:P], sT[:, 0:P])
                dve.tensor_copy(W2T[:, :], sT[:, P:2 * P])
                whhT = sT[:, T_WHH * P:(T_WHH + 3) * P]
                dve.tensor_copy(gru_w[:, 0, STEPS], whhT).then_inc(p_hi, 1)
                dve.wait_ge(p_hi, 1)
                dve.tensor_tensor(gru_w[:, 1, STEPS], whhT, gru_w[:, 0, STEPS].bitcast(F32), ALU.subtract)

            def prepare_more(g, q, _):
                if not isinstance(g, int) or g > 0:
                    return
                for l in range(STEPS):
                    dve.wait_ge(p_ahi, l + 1)
                    dve.tensor_tensor(gru_w[:, 1, l], ps[:, l, 0:3 * P], gru_w[:, 0, l].bitcast(F32), ALU.subtract)
                for k in range(2):
                    dve.wait_ge(p_ahi, STEPS + k + 1)
                    s = slice(512 * k, 512 * k + 512)
                    dve.tensor_tensor(G[:, 1, s], ps[:, 6 + k], G[:, 0, s].bitcast(F32), ALU.subtract)
                dve.wait_ge(p_mm, STEPS + 3)
                dve.wait_ge(w_small, 16 * len(W_SMALL))
                dve.tensor_copy(W0e[:, P:P + 2], ps[:, 5, 0:2])
                dve.tensor_copy(c0[:, :], ps[:, 5, 2:4]).then_inc(p_hi, 1)
                dve.wait_ge(p_hi, 2)
                dve.tensor_tensor(c0[:, 0:1], c0[:, 0:1], ab[:, :], ALU.add)
                wqk = ps[:, 5, 8:8 + 2 * HEADS].rearrange("p (h t) -> p t h", t=2)
                for k in range(4):
                    dve.tensor_copy(Wkq[:, k * LOW:k * LOW + HEADS], wqk[:, 1 - k // 2])
                for rows, col, bias in ((slice(0, LOW + HEADS), 32, r_kb), (slice(QK, KQ), 33, r_qb)):
                    dve.tensor_tensor(ckq[rows], ps[rows, 5, col:col + 1], bias[rows], ALU.add)
                last = dve.tensor_tensor(ce[:, :], ps[:, 5, 128:256], ce[:, :], ALU.add)
                last.then_inc(p_done, 1)
                dve.wait_ge(p_done, 1)

                for b in range(2):
                    last = dve.memset(Y_s[b][:, :, P + 1:P + 2], 1.0)
                last.then_inc(a_ycol, 1)

            def take_edges(g, q, _):
                dve.wait_ge(a_ld[q], (g - q) * 4 + 16)
                dve.tensor_scalar(edges[:, g], adj4[:, q], 0.0, None, ALU.not_equal).then_inc(a_edges, 1)

            def finish(g, b, _):
                dve.wait_ge(a_agg, g + 1)
                agg = ps[:, 4:6, :].rearrange("p k (j e) -> p k j e", e=256)
                den = small[:, b, 2].rearrange("p (k j) -> p k j", j=2)
                dve.tensor_copy(den, agg[:, :, :, P])
                dve.tensor_scalar(deg[:, g].rearrange("p (k j) -> p k j", j=2), agg[:, :, :, P + 1], 1.0, None,
                                  ALU.add).then_inc(a_s3, 1)
                dve.wait_ge(a_s3, 2 * g + 1)
                dve.tensor_tensor(small[:, b, 2], small[:, b, 2], ef[:, g], ALU.mult).then_inc(a_s1, 1)
                dve.wait_ge(a_s1, g + 1)
                dve.reciprocal(small[:, b, 3], small[:, b, 2]).then_inc(a_s2, 1)
                dve.wait_ge(a_s2, g + 1)
                dve.tensor_tensor(small[:, b, 4], small[:, b, 3], ef[:, g], ALU.mult).then_inc(a_s3, 1)
                dve.wait_ge(a_s3, 2 * g + 2)
                dve.wait_ge(a_xb, g + 1)
                for j in range(GW):
                    last = dve.scalar_tensor_tensor(x_all[:, g, j], ps[:, 4 + j // 2, (j % 2) * 256:(j % 2) * 256 + P],
                                                    small[:, b, 4, j:j + 1], xb_s[:, b, j], ALU.mult, ALU.add)
                last.then_inc(a_x1, 1)

            def keep_gT(g, q, _):
                dve.wait_ge(b_g, g + 1)
                dve.tensor_copy(gT_all[:, g], ps[:, 1]).then_inc(b_gT, 1)

            sweep(dve, (1, [(2, prepare), (4, by_pairs(ln_stats(A_PH, lambda g, b: dve.wait_ge(x_ld[b], (g - b) * 8 + 16)))),
                            (-2, by_pairs(finish)), (3, by_pairs(ln_shift(A_PH))), (0, take_edges), (2, prepare_more)]),
                  (1, [(4, by_pairs(ln_stats(B_PH, lambda g, b: dve.wait_ge(a_x1, g + 1)))),
                       (3, by_pairs(ln_shift(B_PH))), (1, keep_gT)]), ring=4)

            def split_h(g, b, l):
                t = g + NG * l
                if l == 0:
                    dve.wait_ge(a_hT, NG + g + 1)
                else:
                    dve.wait_ge(c_hk, t - NG + 1)
                back(dve, c_z, t - 1)
                if l < STEPS - 1:
                    dve.tensor_copy(split[:, b, 0], hT_all[:, g]).then_inc(c_hhi, 1)
                dve.wait_ge(c_hhi, t + 1)
                dve.tensor_tensor(split[:, b, 1], hT_all[:, g], split[:, b, 0].bitcast(F32),
                                  ALU.subtract).then_inc(c_hsp, 1)

            def low_g(g, b, l):
                t = g + NG * l
                dve.wait_ge(c_ghi, t + 1)
                dve.tensor_tensor(split[:, b, 3], gT_all[:, g], split[:, b, 2].bitcast(F32),
                                  ALU.subtract).then_inc(c_glo, 1)

            def new_state(g, b, l):
                t = g + NG * l
                dve.wait_ge(c_zd, t + 1)
                back(dve, c_T, t - 1)
                if l < STEPS - 1:
                    back(dve, c_hk, t - 1)
                else:
                    dve.wait_ge(c_hk, NG * (STEPS - 1))
                dve.tensor_tensor(new_hT[:, b], cand_n[:, b], diff[:, b], ALU.add).then_inc(c_h, 1)

            def candidate(g, b, l):
                t = g + NG * l
                dve.wait_ge(c_sr, t + 1)
                dve.wait_ge(c_hn, t + 1)
                back(dve, c_n, t - 1)
                tt = flat(pre_n[:, b])
                dve.scalar_tensor_tensor(tt, ps[:, 1], gate_b[:, 3:4], flat(gate_r[:, b]),
                                         ALU.add, ALU.mult).then_inc(c_t1, 1)
                dve.wait_ge(c_t1, t + 1)
                dve.wait_ge(c_in, t + 1)
                dve.tensor_tensor(tt, ps[:, 2], tt, ALU.add).then_inc(c_t2, 1)

            def to_x(g, b, l):
                if l < STEPS - 1:
                    return
                t = g + NG * l
                dve.wait_ge(c_T, t + 1)
                for j in range(GW):
                    o = g * GW + j
                    m = maskT[:, bass.ds(o, 1)]
                    last = dve.scalar_tensor_tensor(x_all[:, g, j], ps[:, 4 + b, j * P:(j + 1) * P], m,
                                                    x_all[:, g, j], ALU.mult, ALU.add)
                last.then_inc(c_x2, 1)

            def add_self(g, b, _):
                dve.wait_ge(d_T, g + 1)
                back(dve, d_HT, g - 1)
                dve.tensor_tensor(adjTd_s[:, b], ps[:, 6 + b].rearrange("p (j e) -> p j e", e=P), bcast(ident[:, :]),
                                  ALU.add).then_inc(d_adjT, 1)

            def relu_add(g, b, _):
                dve.wait_ge(d_t1, g + 1)
                dve.scalar_tensor_tensor(x_all[:, g], hT_all[:, g].rearrange("p (j e) -> p j e", e=P), 0.0, x_all[:, g],
                                         ALU.max, ALU.add).then_inc(d_x3, 1)

            sweep(dve, (STEPS, [(1, split_h), (0, candidate), (-1, new_state), (1, low_g), (-3, to_x)]),
                  (1, [(2, ln_stats(D_PH, lambda g, b: dve.wait_ge(c_x2, g + 1))), (-5, relu_add), (0, add_self),
                       (1, ln_shift(D_PH, True))]),
                  (2 / NG, [(2, ln_stats(E_PH, lambda g, b: dve.wait_ge(d_x3, g + 1))), (1, ln_shift(E_PH))]))

            def mask_max(g, b, h):
                u = g * HEADS + h
                q = h % 2
                dve.wait_ge(u_S, u + 1)
                if h == 0:
                    dve.wait_ge(e_M, g + 1)
                alone(dve, dve_met)
                for j in range(GW):
                    last = dve.tensor_tensor_reduce(X_u[:, h % 4, j], ps[:, q, j * P:(j + 1) * P], M_s[:, b, j], 1.0,
                                                    -3.0e38, ALU.add, ALU.max, sm(h, 0)[:, j:j + 1])
                last.then_inc(u_X, 1)
                dve.wait_ge(u_X, u + 1)
                if h % 2:
                    dve.tensor_scalar(sm(h, 0), sm(h, 0), -1.0, None, ALU.mult).then_inc(u_neg, 1)
                dve.scalar_tensor_tensor(X_u[:, h % 4], X_u[:, h % 4], SLOPE, X_u[:, h % 4], ALU.mult, ALU.max)
                if h % 2:
                    dve.wait_ge(u_neg, g * (HEADS // 2) + h // 2 + 1)
                dve.scalar_tensor_tensor(sm(h, 1), sm(h, 0), SLOPE, sm(h, 0), ALU.mult,
                                         ALU.min if h % 2 else ALU.max).then_inc(u_Y, 1)

            def row_sums(g, b, h):
                u = g * HEADS + h
                dve.wait_ge(u_E, u + 1)
                if h % 2 == 0:
                    dve.tensor_reduce(sm(h, 2), E_u[:, h % 4], AX.X, ALU.add).then_inc(u_s, 1)
                    dve.wait_ge(u_s, g * (HEADS // 2) + h // 2 + 1)
                dve.reciprocal(sm(h, 3), sm(h, 2)).then_inc(u_r, 1)

            def to_out(g, b, h):
                if h == HEADS - 1:
                    dve.wait_ge(u_AV, g * HEADS + HEADS)
                    dve.wait_ge(e_hc, g + 1)
                    back(dve, e_th, g - 1)
                    dve.tensor_tensor(o_s[:, b], ps[:, 4 + b], hc_s[:, b], ALU.add).then_inc(e_o, 1)

            stats_e = ln_stats(E_PH, lambda g, b: dve.wait_ge(d_x3, g + 1))
            shift_e = ln_shift(E_PH)

            def split_rows(hi_sem, done, rows_hi, rows_full, n, g):
                dve.tensor_copy(rows_hi[0:n], rows_full[0:n]).then_inc(hi_sem, 1)
                dve.wait_ge(hi_sem, g + 1)
                dve.tensor_tensor(rows_hi[LOW:n], rows_full[LOW:n], rows_hi[LOW:n].bitcast(F32),
                                  ALU.subtract).then_inc(done, 1)

            def group(g, b):
                for h in range(HEADS):
                    if h == 3 and ahead(g):
                        shift_e(g + 2, b, 0)
                    units(g, b, h, [(7, to_out), (3, row_sums), (0, mask_max)])
                    if h == 4 and has(g + 1):
                        back(dve, u_S, g * HEADS)
                        dve.wait_ge(e_kb, g + 2)
                        split_rows(e_khi, e_K, split[:, 1 - b, 2], flat(kf_s[:, 1 - b]), LOW + HEADS, g + 1)
                    if h == 6 and has(g + 1):
                        dve.wait_ge(e_ql[1 - b], (g + b) * 16 + 32)
                        split_rows(e_qhi, e_Q, split[:, 1 - b, 3, 0:P], qf_s[:, 1 - b, 0:P], 2 * LOW, g + 1)
                    if h == 0 and ahead(g):
                        stats_e(g + 2, b, 0)

            all_groups(dve, group)

        @block.scalar
        def _(act):
            for dst, src in W_ROWS:
                act.dma_start(dst, src).then_inc(w_first, 16)
            act.dma_start(*W_FP).then_inc(w_fp, 16)

            def ln_apply(ph, dst, free, scale=None):
                def stage(g, b, _):
                    t = g + NG * ph
                    act.wait_ge(ln_nmr, t + 1)
                    free(t)
                    s = rstd[:, b] if scale is None else small[:, b, 7]
                    for j in range(GW):
                        last = act.activation(dst[:, b, j], x_all[:, g, j], ACT.Relu, bias=nmr[:, b, j:j + 1],
                                              scale=s[:, j:j + 1])
                    last.then_inc(ln_h, 1)
                return stage

            def prepare(g, b, _):
                if not isinstance(g, int) or g > 0:
                    return
                for k in range(1, TB, 2):
                    act.wait_ge(p_T, k + 1)
                    n = min(vec0 + 19, 512 * k + 512) - 512 * k
                    act.activation(sT[:, 512 * k:512 * k + n], ps[:, k, 0:n], ACT.Copy).then_inc(p_TcA, 1)
                for l in range(STEPS):
                    act.wait_ge(p_mm, l + 1)
                    act.activation(gru_w[:, 0, l], ps[:, l, 0:3 * P], ACT.Copy).then_inc(p_ahi, 1)
                for k in range(2):
                    act.wait_ge(p_mm, STEPS + k + 1)
                    act.activation(G[:, 0, 512 * k:512 * k + 512], ps[:, 6 + k], ACT.Copy).then_inc(p_ahi, 1)

            def keep_T(g, b, layer=0):
                t = g + NG * layer
                act.wait_ge(a_T, t + 1)
                if layer == 0:
                    back(act, a_proj, g - 1)
                dst = flat(hT_s[:, b]) if layer == 0 else hT_all[:, g]
                act.activation(dst, ps[:, 0], ACT.Copy).then_inc(a_hT, 1)

            def keep_adjT(g, b, _):
                act.wait_ge(a_Ta, g + 1)
                back(act, a_agg, g - 1)
                act.activation(adjT_s[:, b], ps[:, 1].rearrange("p (j e) -> p j e", e=P), ACT.Copy).then_inc(a_adjT, 1)

            def exps(g, b, _):
                act.wait_ge(a_proj, g + 1)
                fe = ps[:, 2 + 4 * b:4 + 4 * b, :].rearrange("p k (j e) -> p k j e", e=256)
                act.activation(ef[:, g].rearrange("p (k j) -> p k j", j=2), fe[:, :, :, P], ACT.Exp,
                               bias=c0[:, 0:1])
                back(act, a_agg, g - 1)
                act.activation(Y_s[b][:, :, P].rearrange("p (k j) -> p k j", j=2), fe[:, :, :, P + 1], ACT.Exp,
                               bias=c0[:, 1:2]).then_inc(a_exp, 1)
                act.wait_ge(a_exp, g + 1)
                for j in range(GW):
                    last = act.activation(Y_s[b][:, j, 0:P], ps[:, 2 + 4 * b + j // 2, (j % 2) * 256:(j % 2) * 256 + P],
                                          ACT.Copy, scale=Y_s[b][:, j, P:P + 1])
                last.then_inc(a_Y, 1)

            def free_h(t):
                back(act, a_T, t - 1)

            def aggregated(g, b, _):
                back(act, b_g, g - 1)

            sweep(act, (1, [(2, prepare), (0, keep_adjT), (1, lambda g, b, _: keep_T(g, b, 0)), (0, exps), (3, ln_apply(A_PH, h_s, free_h))]),
                  (1, [(1, lambda g, b, _: keep_T(g, b, 1)), (3, aggregated), (3, ln_apply(B_PH, h_s, free_h))]))

            def high_h(g, b, l):
                if l < STEPS - 1:
                    return
                t = g + NG * l
                act.wait_ge(c_hk, t - NG + 1)
                back(act, c_z, t - 1)
                act.activation(split[:, b, 0], hT_all[:, g], ACT.Copy).then_inc(c_hhi, 1)

            def high_g(g, b, l):
                t = g + NG * l
                if l == 0:
                    act.wait_ge(b_gT, g + 1)
                else:
                    act.wait_ge(c_gk, t - NG + 1)
                back(act, c_z, t - 1)
                act.activation(split[:, b, 2], gT_all[:, g], ACT.Copy).then_inc(c_ghi, 1)

            def reset(g, b, l):
                t = g + NG * l
                act.wait_ge(c_r, t + 1)
                back(act, c_t1, t - 1)
                act.activation(flat(gate_r[:, b]), ps[:, 0], ACT.Sigmoid,
                               bias=gate_b[:, 0:1]).then_inc(c_sr, 1)

            def candidate_and_update(g, b, l):
                t = g + NG * l
                act.wait_ge(c_t2, t + 1)
                back(act, c_h, t - 1)
                act.activation(cand_n[:, b], pre_n[:, b], ACT.Tanh, bias=gate_b[:, 2:3]).then_inc(c_n, 1)
                act.wait_ge(c_z, t + 1)
                back(act, c_zd, t - 1)
                act.activation(flat(gate_z[:, b]), ps[:, 3], ACT.Sigmoid,
                               bias=gate_b[:, 1:2]).then_inc(c_sz, 1)

            def keep_h(g, b, l):
                if l == STEPS - 1:
                    return
                t = g + NG * l
                act.wait_ge(c_h, t + 1)
                act.activation(hT_all[:, g], flat(new_hT[:, b]), ACT.Copy).then_inc(c_hk, 1)

            def keep_nat(g, b, l):
                t = g + NG * l
                if l < STEPS - 1:
                    act.wait_ge(c_T, t + 1)
                    back(act, c_g, t - 1)
                    act.activation(flat(new_h[:, b]), ps[:, 4 + b], ACT.Copy).then_inc(c_nat, 1)

            def keep_g(g, b, l):
                if l == STEPS - 1:
                    return
                t = g + NG * l
                act.wait_ge(c_g, t + 1)
                act.activation(gT_all[:, g], ps[:, 6 + b], ACT.Copy).then_inc(c_gk, 1)



            def keep_HT(g, b, _):
                act.wait_ge(d_HT, g + 1)
                back(act, d_o, g - 1)
                act.activation(flat(HTd_s[:, b]), ps[:, 2 + b], ACT.Copy).then_inc(d_HTk, 1)

            def scale_o(g, b, _):
                act.wait_ge(d_o, g + 1)
                for j in range(GW):
                    last = act.activation(hT_all[:, g, j * P:(j + 1) * P], ps[:, b, j * P:(j + 1) * P], ACT.Copy,
                                          scale=deg[:, g, j:j + 1])
                last.then_inc(d_t, 1)

            sweep(act, (STEPS, [(1, high_h), (-2, keep_nat), (0, reset), (-3, keep_g), (1, high_g), (0, candidate_and_update), (-1, keep_h)]),
                  (1, [(-2, keep_HT), (0, ln_apply(D_PH, hd_s, lambda t: back(act, d_HT, t - NG * D_PH - 1), True)), (-3, scale_o)]),
                  (2 / NG, [(0, ln_apply(E_PH, he_s, lambda t: None))]))

            def exponent(g, b, h):
                u = g * HEADS + h
                back(act, u_P, u - 3)
                if h % 2:
                    act.wait_ge(u_Y, u + 1)
                    for j in range(GW):
                        last = act.activation(E_u[:, h % 4, j], X_u[:, h % 4, j], ACT.Exp, bias=sm(h, 1)[:, j:j + 1],
                                              accum_out=sm(h, 2)[:, j:j + 1])
                    last.then_inc(u_E, 1)
                else:
                    act.wait_ge(u_Z, g * (HEADS // 2) + h // 2 + 1)
                    act.activation(E_u[:, h % 4], X_u[:, h % 4], ACT.Exp).then_inc(u_E, 1)

            def keep_A(g, b, h):
                u = g * HEADS + h
                act.wait_ge(u_T, u + 1)
                back(act, u_AV, u - 3)
                act.activation(flat(A_u[:, h % 4]), ps[:, 2 + h % 2], ACT.Copy).then_inc(u_A, 1)

            def tanh(g, b, h):
                if h == HEADS - 1:
                    act.wait_ge(e_o, g + 1)
                    back(act, e_sg, g - 1)
                    act.activation(t_s[:, b], o_s[:, b], ACT.Tanh, scale=0.5).then_inc(e_th, 1)

            def keep_V(g, b, c):
                act.wait_ge(e_V, g * HEADS + c + 1)
                if isinstance(g, int) and g == 0 and c == 0:
                    act.wait_ge(d_x3, NG)
                back(act, u_AV, (g - 1) * HEADS)
                act.activation(V[:, b, c // 2, (c % 2) * 512:(c % 2) * 512 + 512], ps[:, 7 - c % 2],
                               ACT.Copy).then_inc(e_Vk, 1)

            def apply_e(g, b, graphs):
                t = g + NG * E_PH
                if graphs[0] == 0:
                    act.wait_ge(ln_nmr, t + 1)
                    back(act, e_hc, g - 1)
                    back(act, e_T, g - 1)
                for j in graphs:
                    last = act.activation(he_s[:, b, j], x_all[:, g, j], ACT.Relu, bias=nmr[:, b, j:j + 1],
                                          scale=rstd[:, b, j:j + 1])
                if graphs[-1] == GW - 1:
                    last.then_inc(ln_h, 1)

            def group(g, b):
                for h in range(HEADS):
                    value_chunk(g, b, h, keep_V, 1)
                    units(g, b, h, [(5, keep_A), (2, exponent), (7, tanh)])
                    if h == 0 and has(g + 1):
                        act.wait_ge(e_T, g + 2)
                        back(act, e_split, g)
                        back(act, e_k, g)
                        act.activation(flat(heT_s[:, 1 - b]), ps[:, 4 + b], ACT.Copy).then_inc(e_hT, 1)
                        back(act, e_V, HEADS * g)
                        act.wait_ge(e_hT, g + 2)
                        act.activation(split[:, 1 - b, 0], flat(heT_s[:, 1 - b]), ACT.Copy).then_inc(e_hhi, 1)
                    if h == 2 and has(g + 1):
                        act.wait_ge(e_k, g + 2)
                        back(act, e_K, g)
                        back(act, e_Q, g)
                        act.activation(flat(kf_s[:, 1 - b])[0:KQ], ps[0:KQ, 4 + b], ACT.Identity,
                                       bias=ckq[0:KQ]).then_inc(e_kb, 1)
                    if h == 4 and ahead(g):
                        apply_e(g + 2, b, (0, 1))
                    if h == 6 and ahead(g):
                        apply_e(g + 2, b, (2, 3))

            all_groups(act, group)

        @block.tensor
        def _(pe):
            pe.wait_ge(w_first, 16 * (len(W_FIRST) + len(W_ROWS)))
            pe.wait_ge(p_id, 1)
            for k, tile in enumerate(tiles):
                if k == T_GW:
                    pe.wait_ge(w_gru, 16 * len(W_GRU))
                n = tile.shape[0]
                last = pe.transpose(ps[:, k // 4, (k % 4) * P:(k % 4) * P + n], tile, ident[0:n, 0:n])
                if k % 4 == 3 or k == NT - 1:
                    last.then_inc(p_T, 1)
            pe.wait_ge(p_Tc, TB // 2)
            pe.wait_ge(p_TcA, TB // 2)

            def tT(k):
                return sT[:, k * P:(k + 1) * P]

            for l in range(STEPS):
                pe.matmul(ps[:, l, 0:3 * P], tT(T_GW + l), sT[:, T_WIH * P:(T_WIH + 3) * P], start=True,
                          stop=True).then_inc(p_mm, 1)
            pe.wait_ge(w_fp, 16)
            for h in range(HEADS):
                last = pe.matmul(ps[:, 6 + h // 4, (h % 4) * P:(h % 4) * P + P], tT(T_FC + h), r_fp[:, h],
                                 start=True, stop=True)
                if h % 4 == 3:
                    last.then_inc(p_mm, 1)
            pe.wait_ge(p_bld, 1)
            pe.matmul(ps[:, 5, 0:2], r_w0, r_a, start=True, stop=True)
            pe.matmul(ps[:, 5, 2:4], b0rep, r_a, start=True, stop=True)
            for h in range(HEADS):
                pe.matmul(ps[:, 5, 8 + 2 * h:10 + 2 * h], tT(T_FC + h), r_qk, start=True, stop=True)
            for col in range(2):
                pe.matmul(ps[0:KQ, 5, 32 + col:33 + col], fcbkq, r_qk[:, 1 - col:2 - col], start=True, stop=True)
            for h in range(HEADS):
                last = pe.matmul(ps[:, 5, 128:256], fcbrep[:, h], r_fp[:, h], start=(h == 0), stop=(h == HEADS - 1))
            last.then_inc(p_mm, 1)
            pe.wait_ge(p_done, 1)
            pe.wait_ge(a_ycol, 1)

            def transposes(g, b, layer=0):
                t = g + NG * layer
                pe.wait_ge(ln_h, t + 1)
                back(pe, a_hT, t)
                for j in range(GW):
                    last = pe.transpose(ps[:, 0, j * P:(j + 1) * P], h_s[:, b, j], ident[:, :])
                last.then_inc(a_T, 1)

            def adj_transposes(g, q, _):
                pe.wait_ge(a_ld[q], (g - q) * 4 + 16)
                back(pe, a_adjT, g)
                for j in range(GW):
                    last = pe.transpose(ps[:, 1, j * P:(j + 1) * P], adj4[:, q, j], ident[:, :])
                last.then_inc(a_Ta, 1)

            def project(g, b, _):
                pe.wait_ge(a_hT, g + 1)
                back(pe, a_Y, g - 1)
                for j in range(GW):
                    o = (j % 2) * 256
                    last = pe.matmul(ps[:, 2 + 4 * b + j // 2, o:o + P + 2], hT_s[:, b, j], W0e[:, :], start=True, stop=True)
                last.then_inc(a_proj, 1)

            def aggregate(g, b, _):
                pe.wait_ge(a_Y, g + 1)
                pe.wait_ge(a_adjT, g + 1)
                back(pe, a_x1, g)
                for j in range(GW):
                    o = (j % 2) * 256
                    last = pe.matmul(ps[:, 4 + j // 2, o:o + P + 2], adjT_s[:, b, j], Y_s[b][:, j], start=True, stop=True)
                last.then_inc(a_agg, 1)

            def b_agg(g, b, _):
                pe.wait_ge(a_edges, g + 1)
                if isinstance(g, int) and g == 0:
                    pe.wait_ge(a_adjT, NG)
                back(pe, b_gT, g)
                for j in range(GW):
                    last = pe.matmul(ps[:, 1, j * P:(j + 1) * P], h_s[:, b, j], edges[:, g, j], start=True, stop=True)
                last.then_inc(b_g, 1)

            sweep(pe, (1, [(1, adj_transposes), (2, lambda g, q, _: transposes(g, q % 2, 0)), (-1, by_pairs(aggregate)),
                           (1, by_pairs(project))]),
                  (1, [(2, lambda g, q, _: transposes(g, q % 2, 1)), (2, by_pairs(b_agg))]), ring=4)

            def three(bank, w, col, src, b, start, stop, l):
                hi, lo = gru_w[:, 0, w, col * P:(col + 1) * P], gru_w[:, 1, w, col * P:(col + 1) * P]
                pe.matmul(ps[:, bank], hi, split[:, b, src], start=start, stop=False)
                pe.matmul(ps[:, bank], lo, split[:, b, src], start=False, stop=False)
                return pe.matmul(ps[:, bank], hi, split[:, b, src + 1], start=False, stop=stop)

            def gate_products(g, b, l):
                t = g + NG * l
                pe.wait_ge(c_hsp, t + 1)
                back(pe, c_sr, t)
                if l == 0:
                    pe.wait_ge(a_hT, 2 * NG)
                    pe.wait_ge(b_gT, NG)
                three(0, STEPS, 0, 0, b, True, False, l)
                pe.wait_ge(c_glo, t + 1)
                three(0, l, 0, 2, b, False, True, l).then_inc(c_r, 1)
                back(pe, c_t1, t)
                three(1, STEPS, 2, 0, b, True, True, l).then_inc(c_hn, 1)
                back(pe, c_t2, t)
                three(2, l, 2, 2, b, True, True, l).then_inc(c_in, 1)
                back(pe, c_sz, t)
                three(3, STEPS, 1, 0, b, True, False, l)
                three(3, l, 1, 2, b, False, True, l).then_inc(c_z, 1)

            def c_trans(g, b, l):
                t = g + NG * l
                pe.wait_ge(c_h, t + 1)
                if l < STEPS - 1:
                    back(pe, c_nat, t - 1)
                else:
                    pe.wait_ge(c_nat, NG * (STEPS - 1))
                    back(pe, c_x2, g - 1)
                for j in range(GW):
                    last = pe.transpose(ps[:, 4 + b, j * P:(j + 1) * P], new_hT[:, b, j], ident[:, :])
                last.then_inc(c_T, 1)

            def step_trans(g, b, l):
                if l < STEPS - 1:
                    c_trans(g, b, l)

            def last_trans(g, b, l):
                if l == STEPS - 1:
                    c_trans(g, b, l)

            def c_agg(g, b, l):
                if l == STEPS - 1:
                    return
                t = g + NG * l
                pe.wait_ge(c_nat, t + 1)
                if l == 0:
                    pe.wait_ge(b_gT, NG)
                back(pe, c_gk, t - 1)
                for j in range(GW):
                    last = pe.matmul(ps[:, 6 + b, j * P:(j + 1) * P], new_h[:, b, j], edges[:, g, j], start=True, stop=True)
                last.then_inc(c_g, 1)


            def d_trans(g, b, _):
                pe.wait_ge(d_ld[b], (g - b) * 8 + 16)
                back(pe, d_adjT, g - 1)
                if isinstance(g, int) and g == 0:
                    pe.wait_ge(c_gk, NG * (STEPS - 1))
                for j in range(GW):
                    last = pe.transpose(ps[:, 6 + b, j * P:(j + 1) * P], adj4[:, b, j], ident[:, :])
                last.then_inc(d_T, 1)

            def d_agg(g, b, _):
                pe.wait_ge(d_adjT, g + 1)
                pe.wait_ge(ln_h, NG * D_PH + g + 1)
                back(pe, d_HTk, g - 1)
                if isinstance(g, int) and g == 0:
                    pe.wait_ge(c_t2, NG * STEPS)
                    pe.wait_ge(c_sz, NG * STEPS)
                for j in range(GW):
                    last = pe.matmul(ps[:, 2 + b, j * P:(j + 1) * P], hd_s[:, b, j], adjTd_s[:, b, j], start=True, stop=True)
                last.then_inc(d_HT, 1)

            def d_project(g, b, _):
                pe.wait_ge(d_HTk, g + 1)
                back(pe, d_t, g - 1)
                for j in range(GW):
                    last = pe.matmul(ps[:, b, j * P:(j + 1) * P], HTd_s[:, b, j], W2T[:, :], start=True, stop=True)
                last.then_inc(d_o, 1)

            sweep(pe, (STEPS, [(0, gate_products), (-2, c_agg), (-2, last_trans), (-1, step_trans)]),
                  (1, [(1, d_trans), (-1, d_agg), (-2, d_project)]))

            def logits(g, b, h):
                u = g * HEADS + h
                q = h % 2
                if h == 0:
                    pe.wait_ge(e_K, g + 1)
                    pe.wait_ge(e_Q, g + 1)
                back(pe, u_X, u - 1)
                pe.matmul(ps[:, q], split[0:2 * LOW, b, 3, 0:P], along(pick[:, h * GW:(h + 1) * GW]), start=True, stop=False)
                pe.matmul(ps[:, q], selk[:, h], split[0:LOW + HEADS, b, 2], start=False, stop=True).then_inc(u_S, 1)

            def probs_T(g, b, h):
                u = g * HEADS + h
                q = h % 2
                pe.wait_ge(u_P, u + 1)
                back(pe, u_A, u - 1)
                for j in range(GW):
                    last = pe.transpose(ps[:, 2 + q, j * P:(j + 1) * P], P_u[:, h % 4, j], ident[:, :])
                last.then_inc(u_T, 1)

            def attend(g, b, h):
                u = g * HEADS + h
                q = h % 2
                pe.wait_ge(u_A, u + 1)
                if h == 0:
                    pe.wait_ge(e_Vk, (g + 1) * HEADS)
                    back(pe, e_o, g - 1)
                    if has(g + 1):
                        pe.wait_ge(e_kb, g + 2)
                for j in range(GW):
                    last = pe.matmul(ps[:, 4 + b, j * P:(j + 1) * P], A_u[:, h % 4, j], V[:, b, j, h * P:(h + 1) * P],
                                     start=(h == 0 and j == 0), stop=(h == HEADS - 1), skip_group_check=True)
                last.then_inc(u_AV, 1)

            def values(g, b, c):
                pe.wait_ge(e_split, g + 1)
                back(pe, e_Vk, g * HEADS + c - 1)
                j, bank, cols = c // 2, 7 - c % 2, slice((c % 2) * 512, (c % 2) * 512 + 512)
                hi, lo = (split[:, b, k, j * P:(j + 1) * P] for k in range(2))
                pe.matmul(ps[:, bank], hi, G[:, 0, cols], start=True, stop=False)
                pe.matmul(ps[:, bank], lo, G[:, 0, cols], start=False, stop=False)
                pe.matmul(ps[:, bank], hi, G[:, 1, cols], start=False, stop=True).then_inc(e_V, 1)

            def transpose_he(g, b, bank):
                pe.wait_ge(ln_h, NG * E_PH + g + 1)
                for j in range(GW):
                    last = pe.transpose(ps[:, bank, j * P:(j + 1) * P], he_s[:, b, j], ident[:, :])
                last.then_inc(e_T, 1)

            pe.wait_ge(c_x2, NG)
            transpose_he(0, 0, 5)
            pe.wait_ge(d_t, NG)
            pe.wait_ge(d_HTk, NG)
            pe.wait_ge(d_adjT, NG)

            def group(g, b):
                for h in range(HEADS):
                    units(g, b, h, [(0, logits), (5, probs_T), (6, attend)])
                    if h == 1 and has(g + 1):
                        pe.wait_ge(e_hT, g + 2)
                        pe.matmul(ps[0:KQ, 4 + b], Wkq[:, :], flat(heT_s[:, 1 - b]), start=True, stop=True).then_inc(e_k, 1)
                    value_chunk(g, b, h, values)
                    if h == 7 and has(g + 2):
                        back(pe, e_o, g)
                        transpose_he(g + 2, b, 5 - b)

            all_groups(pe, group)


_INS = ["x", "adj", "nodemask", "L0_gnn_W_w", "L0_gnn_W_b", "L0_gnn_a_w", "L0_gnn_a_b", "L1_gnn_weight", "L1_gnn_w_ih",
        "L1_gnn_w_hh", "L1_gnn_b_ih", "L1_gnn_b_hh", "L2_gnn_W", "L2_gnn_b", "L3_gnn_fc_w", "L3_gnn_fc_b", "L3_gnn_q_w",
        "L3_gnn_q_b", "L3_gnn_k_w", "L3_gnn_k_b", "L3_gnn_fp_w", "L3_gnn_fp_b"]


def kernel(**inputs):
    import numpy as _np
    import concourse.bacc as _bacc
    from concourse import mybir as _mybir
    from concourse.bass_utils import run_bass_kernel_spmd as _run

    nc = _bacc.Bacc("TRN2", target_bir_lowering=False, num_devices=1)
    arrays, args = {}, []
    for name in _INS:
        a = _np.ascontiguousarray(inputs[name])
        arrays[f"in_{name}"] = a
        args.append(nc.dram_tensor(f"in_{name}", a.shape, _mybir.dt.from_np(a.dtype), kind="ExternalInput").ap())
    o = nc.dram_tensor("out_x", (GRAPHS, P, P), F32, kind="ExternalOutput").ap()
    build(nc, *args, o)
    r = _run(nc, [arrays], core_ids=[0])
    return r.results[0]["out_x"]
```
